# Optimizing a Trainium2 kernel written in Bass

```python
import numpy as np
import jax
import jax.numpy as jnp

def _softmax(x, axis=-1):
    return jax.nn.softmax(x, axis=axis)

def _gelu(x):
    return jax.nn.gelu(x, approximate=True)

def _silu(x):
    return jax.nn.silu(x)

def _sigmoid(x):
    return jax.nn.sigmoid(x)

def _layernorm(x, axis=-1, eps=1e-05):
    m = jnp.mean(x, axis=axis, keepdims=True)
    v = jnp.var(x, axis=axis, keepdims=True)
    return (x - m) / jnp.sqrt(v + eps)

def _scatter_add(tgt, idx, src, axis=0):
    return tgt.at[idx].add(src)

def _segment_sum(src, seg, n):
    return jax.ops.segment_sum(src, seg, n)
kernel_name = 'mk_adj_ffn_d2_adj_r2_f85c8d'

def setup_inputs(seed: int=0):
    np.random.seed(seed)
    _w = jnp.asarray

    def _rec_inputs():
        import jax
        import jax.numpy as jnp
        _gk = jax.random.key(seed)
        x = -0.0006008 + 1.001 * jax.random.normal(jax.random.fold_in(_gk, 1), (4096, 128), jnp.float32)
        _w = (1.0 + jnp.arange(4096, dtype=jnp.float32)) ** (-0.5)
        _w = _w / _w.mean()
        _pij = jnp.clip(0.00390625 * _w[:, None] * _w[None, :], 0.0, 1.0)
        _a = jax.random.uniform(jax.random.fold_in(_gk, 2), (4096, 4096)) < _pij
        _a = jnp.logical_or(_a, jnp.eye(4096, dtype=bool))
        _af = _a.astype(jnp.float32)
        _af = _af * jax.random.uniform(jax.random.fold_in(_gk, 3), (4096, 4096), jnp.float32, 0.05, 1)
        adj = _af
        return (x, adj)
    x, adj = _rec_inputs()

    def _L0_gnn_setup():
        import jax, jax.numpy as jnp
        import numpy as np
        N = 5000
        F = 128
        key = jax.random.key(seed)
        k1, k2 = jax.random.split(key)
        x = jax.random.normal(k1, (N, F), dtype=jnp.float32)
        A = jax.random.uniform(k2, (N, N), dtype=jnp.float32)
        W = jnp.ones((F,), dtype=jnp.float32)
        return {'input': x, 'A': A, 'W': W}
    _L0_gnn_all = _L0_gnn_setup()
    _L0_gnn_in = {k: v for k, v in _L0_gnn_all.items() if k in ('W',)}
    del _L0_gnn_all

    def _L0_ffn_setup():
        import jax, jax.numpy as jnp
        import numpy as np
        IN_CH = 128
        OUT_CH = 128
        key = jax.random.key(seed)
        kx, kw, kb = jax.random.split(key, 3)
        x = jax.random.normal(kx, (8, 2048, IN_CH), dtype=jnp.float32)
        bound = 1.0 / np.sqrt(IN_CH)
        weight = jax.random.uniform(kw, (OUT_CH, IN_CH), dtype=jnp.float32, minval=-bound, maxval=bound)
        bias = jax.random.uniform(kb, (OUT_CH,), dtype=jnp.float32, minval=-bound, maxval=bound)
        return {'x': x, 'weight': weight, 'bias': bias}
    _L0_ffn_all = _L0_ffn_setup()
    _L0_ffn_in = {k: v for k, v in _L0_ffn_all.items() if k in ('weight', 'bias')}
    del _L0_ffn_all

    def _L1_gnn_setup():
        import jax, jax.numpy as jnp
        import numpy as np
        N = 4096
        D = 128
        CUTOFF = 1.0
        MU = 1.0
        SIGMA = 0.5

        def sensitivity(r, mu, sigma):
            return jnp.exp(-(1.0 / r - 1.0 / mu) ** 2 / (2.0 * sigma * sigma))
        key = jax.random.key(seed)
        k_z, k_d, k_w = jax.random.split(key, 3)
        z = jax.random.normal(k_z, (N, D), dtype=jnp.float32)
        dist_matrix = jax.random.uniform(k_d, (N, N), dtype=jnp.float32) * 2.0 + 0.05
        W = jax.random.normal(k_w, (D, D), dtype=jnp.float32)
        B = jnp.zeros((D,), dtype=jnp.float32)
        return {'z': z, 'dist_matrix': dist_matrix, 'W': W, 'B': B}
    _L1_gnn_all = _L1_gnn_setup()
    _L1_gnn_in = {k: v for k, v in _L1_gnn_all.items() if k in ('W', 'B')}
    del _L1_gnn_all

    def _L1_ffn_setup():
        import jax, jax.numpy as jnp
        import numpy as np
        B, S, D, H, E, K = (8, 4096, 128, 512, 8, 2)
        key = jax.random.key(seed)
        ks = jax.random.split(key, 7)
        s_in = 1.0 / np.sqrt(D)
        s_hid = 1.0 / np.sqrt(H)
        return {'x': jax.random.normal(ks[0], (B, S, D), dtype=jnp.float32), 'Wg': jax.random.uniform(ks[1], (E, D), jnp.float32, -s_in, s_in), 'bg': jax.random.uniform(ks[2], (E,), jnp.float32, -s_in, s_in), 'W1': jax.random.uniform(ks[3], (E, H, D), jnp.float32, -s_in, s_in), 'b1': jax.random.uniform(ks[4], (E, H), jnp.float32, -s_in, s_in), 'W2': jax.random.uniform(ks[5], (E, D, H), jnp.float32, -s_hid, s_hid), 'b2': jax.random.uniform(ks[6], (E, D), jnp.float32, -s_hid, s_hid)}
    _L1_ffn_all = _L1_ffn_setup()
    _L1_ffn_in = {k: v for k, v in _L1_ffn_all.items() if k in ('Wg', 'bg', 'W1', 'b1', 'W2', 'b2')}
    del _L1_ffn_all
    return {'x': x, 'adj': adj, 'L0_gnn_W': _L0_gnn_in['W'], 'L0_ffn_weight': _L0_ffn_in['weight'], 'L0_ffn_bias': _L0_ffn_in['bias'], 'L1_gnn_W': _L1_gnn_in['W'], 'L1_gnn_B': _L1_gnn_in['B'], 'L1_ffn_Wg': _L1_ffn_in['Wg'], 'L1_ffn_bg': _L1_ffn_in['bg'], 'L1_ffn_W1': _L1_ffn_in['W1'], 'L1_ffn_b1': _L1_ffn_in['b1'], 'L1_ffn_W2': _L1_ffn_in['W2'], 'L1_ffn_b2': _L1_ffn_in['b2']}

def reference(x, adj, L0_gnn_W, L0_ffn_weight, L0_ffn_bias, L1_gnn_W, L1_gnn_B, L1_ffn_Wg, L1_ffn_bg, L1_ffn_W1, L1_ffn_b1, L1_ffn_W2, L1_ffn_b2):
    import jax
    import jax.numpy as jnp

    def _L0_gnn_ref(input, A, W):
        import jax, jax.numpy as jnp
        import numpy as np
        N = 5000
        F = 128
        hidden = input * W
        return A @ hidden

    def _L0_ffn_ref(x, weight, bias):
        import jax, jax.numpy as jnp
        import numpy as np
        IN_CH = 128
        OUT_CH = 128
        return jnp.einsum('bsi,oi->bso', x, weight) + bias

    def _L1_gnn_ref(z, dist_matrix, W, B):
        import jax, jax.numpy as jnp
        import numpy as np
        N = 4096
        D = 128
        CUTOFF = 1.0
        MU = 1.0
        SIGMA = 0.5

        def sensitivity(r, mu, sigma):
            return jnp.exp(-(1.0 / r - 1.0 / mu) ** 2 / (2.0 * sigma * sigma))
        msg = z @ W + B
        sens = sensitivity(dist_matrix, MU, SIGMA)
        weights = jnp.where(dist_matrix < CUTOFF, sens, 0.0)
        return weights @ msg

    def _L1_ffn_ref(x, Wg, bg, W1, b1, W2, b2):
        import jax, jax.numpy as jnp
        import numpy as np
        B, S, D, H, E, K = (8, 4096, 128, 512, 8, 2)
        gate_scores = jnp.einsum('bsd,ed->bse', x, Wg) + bg
        topk_scores, topk_idx = jax.lax.top_k(gate_scores, K)
        topk_probs = jax.nn.softmax(topk_scores, axis=-1)
        combine = jnp.sum(topk_probs[..., None] * jax.nn.one_hot(topk_idx, E, dtype=x.dtype), axis=-2)
        out = jnp.zeros_like(x)
        for e in range(E):
            h = jax.nn.relu(jnp.einsum('bsd,hd->bsh', x, W1[e]) + b1[e])
            y = jnp.einsum('bsh,dh->bsd', h, W2[e]) + b2[e]
            out = out + combine[..., e:e + 1] * y
        return out
    x = x + _L0_gnn_ref(_layernorm(x, axis=-1), adj, L0_gnn_W)
    x = x + _L0_ffn_ref(_layernorm(x, axis=-1)[None], L0_ffn_weight, L0_ffn_bias)[0]
    x = x + _L1_gnn_ref(_layernorm(x, axis=-1), adj, L1_gnn_W, L1_gnn_B)
    x = x + _L1_ffn_ref(_layernorm(x, axis=-1)[None], L1_ffn_Wg, L1_ffn_bg, L1_ffn_W1, L1_ffn_b1, L1_ffn_W2, L1_ffn_b2)[0]
    return x

_drawn_inputs = setup_inputs


def setup_inputs(seed=0):
    import zlib

    import numpy as np

    out = dict(_drawn_inputs(seed))
    spreads = {'L0_gnn_W': (1.0, 0.2), 'L1_gnn_B': (0.0, 0.1)}
    factors = {'L1_ffn_Wg': 8.0,
     'L1_ffn_bg': 8.0,
     'L1_ffn_W1': 8.0,
     'L1_ffn_b1': 8.0,
     'L1_ffn_W2': 8.0,
     'L1_ffn_b2': 64.0}
    for name, (base, spread) in spreads.items():
        noise = np.random.default_rng([zlib.crc32(name.encode()), seed]).standard_normal(out[name].shape)
        drawn = base * np.exp(spread * noise) if base else spread * noise
        out[name] = jnp.asarray(drawn.astype(out[name].dtype))
    for name, factor in factors.items():
        out[name] = (out[name] * factor).astype(out[name].dtype)
    return out
```

```python
import concourse.bass as bass
from concourse import mybir
from contextlib import ExitStack


def gnn_ffn_gnn_moe_kernel(
    nc: bass.Bass,
    x: bass.AP,
    adjT: bass.AP,
    w_l0: bass.AP,
    ffn_wT: bass.AP,
    ffn_b: bass.AP,
    gnn_w: bass.AP,
    gnn_b: bass.AP,
    gate_wT: bass.AP,
    gate_b: bass.AP,
    w1T: bass.AP,
    b1T: bass.AP,
    w2T: bass.AP,
    b2: bass.AP,
    out: bass.AP,
):
    f32 = mybir.dt.float32
    i32 = mybir.dt.int32
    u32 = mybir.dt.uint32
    ALU = mybir.AluOpType
    ACT = mybir.ActivationFunctionType
    AX = mybir.AxisListType

    P = 128
    D = x.shape[1]
    N = x.shape[0]
    NB = N // P
    C, G = adjT.shape[0], adjT.shape[1]
    T = N // C
    BC = T // P
    J = NB // G
    GT = J * T
    E = gate_b.shape[0]
    HID = b1T.shape[1] // E * P
    K = HID // P
    EPS = 1e-5
    TINY = 2.0 ** -60
    MAGIC = float(0x5F3759DF)
    DVE_RECIP = (1, 5)

    ctx = ExitStack()
    with ctx:
        def sb(name, shape, dt=f32):
            return ctx.enter_context(nc.sbuf_tensor(name, shape, dt))

        def pb(name):
            return ctx.enter_context(nc.psum_tensor(name, [P, 512], f32))

        def sem(name):
            return ctx.enter_context(nc.semaphore(name))

        xs = sb("xs", [P, NB, D])
        h0 = sb("h0", [P, NB, D])
        msg = sb("msg", [P, NB, D])
        ring = sb("ring", [P, G, GT])
        w1_s = sb("w1_s", [P, E * HID])
        w2_s = sb("w2_s", [P, E * K, D])
        ffn_s = sb("ffn_s", [P, D])
        gnn_s = sb("gnn_s", [P, D])
        gate_s = sb("gate_s", [P, E])
        b1_s = sb("b1_s", [P, E * K])
        b2_s = sb("b2_s", [E, D])
        w_row = sb("w_row", [P, D])
        ffnb_row = sb("ffnb_row", [P, D])
        gnnb_row = sb("gnnb_row", [P, D])
        gateb_row = sb("gateb_row", [P, E])
        ident = sb("ident", [P, P])
        iota_e = sb("iota_e", [P, E])
        aggT = sb("aggT", [P, T])
        z = sb("z", [P, BC, D])
        zT = sb("zT", [P, T])
        stats = sb("stats", [P, BC, 6])
        mv = sb("mv", [P, BC, 2])
        va = sb("va", [P, BC])
        hv = sb("hv", [P, BC])
        ya = sb("ya", [P, BC])
        yb = sb("yb", [P, BC])
        sc = sb("sc", [P, BC, E])
        top = sb("top", [P, BC, 8])
        topi = sb("topi", [P, BC, 8], u32)
        topf = sb("topf", [P, BC, 2])
        gap = sb("gap", [P, BC])
        eg = sb("eg", [P, BC])
        den = sb("den", [P, BC])
        pr = sb("pr", [P, BC, 2])
        comb = sb("comb", [P, NB, E])
        comb_c = sb("comb_c", [P, BC, E])
        cj = sb("cj", [P, 2, E])
        combT = sb("combT", [E, BC, P])
        hid = ring[:, :, :].rearrange("p g n -> p (g n)")

        acc = [pb("accA"), pb("accB")]
        pT = pb("pT")
        pF = pb("pF")
        pH = [pb("pH0"), pb("pH1")]
        pY = [pb("pY0"), pb("pY1")]

        s_x = sem("s_x")
        s_par = sem("s_par")
        s_in = [sem(f"s_in{g}") for g in range(G)]
        s_id = sem("s_id")
        s_h0 = sem("s_h0")
        s_grp = sem("s_grp")
        s_half = sem("s_half")
        s_agg = sem("s_agg")
        s_t1 = sem("s_t1")
        s_z1 = sem("s_z1")
        s_t2 = sem("s_t2")
        s_zT = sem("s_zT")
        s_f = sem("s_f")
        s_z2 = sem("s_z2")
        s_t3 = sem("s_t3")
        s_zT2 = sem("s_zT2")
        s_m = sem("s_m")
        s_msg = sem("s_msg")
        s_mask = sem("s_mask")
        s_rec = sem("s_rec")
        s_act = sem("s_act")
        s_wr = sem("s_wr")
        s_gt = sem("s_gt")
        s_gap = sem("s_gap")
        s_eg = sem("s_eg")
        s_zs = sem("s_zs")
        s_comb = sem("s_comb")
        s_cc = sem("s_cc")
        s_ct = sem("s_ct")
        s_cT = sem("s_cT")
        s_hp = sem("s_hp")
        s_hd = sem("s_hd")
        s_hd2 = sem("s_hd2")
        s_y = sem("s_y")
        s_ya = sem("s_ya")
        s_out = sem("s_out")

        block = ctx.enter_context(nc.Block())

        @block.sync
        def _(sp):
            sp.dma_start(xs[:, :, :], x.rearrange("(b p) d -> p b d", p=P)).then_inc(s_x, 16)
            sp.dma_start(w_row[:, :], w_l0.partition_broadcast(P)).then_inc(s_x, 16)
            for g in range(G):
                sp.dma_start(ring[:, g, :], adjT[0, g]).then_inc(s_in[g], 16)
            for half in range(2):
                with sp.Fori(1 - half, C) as c:
                    for g in range(G):
                        sp.wait_ge(s_grp, (c + (half * C - 1)) * G + (g + 1))
                        sp.dma_start(ring[:, g, :], adjT[c, g]).then_inc(s_in[g], 16)
            sp.wait_ge(s_ya, C * (E + 1))
            sp.dma_start(out.rearrange("(b p) d -> p b d", p=P), xs[:, :, :]).then_inc(s_out, 16)
            sp.wait_ge(s_out, 16)

        @block.gpsimd
        def _(pool):
            nc.gpsimd.memset(ident[:, :], 0.0).then_inc(s_id, 1)
            pool.wait_ge(s_id, 1)
            nc.gpsimd.affine_select(out=ident[:, :], in_=ident[:, :], compare_op=ALU.not_equal, fill=1.0,
                                    base=0, pattern=[[-1, P]], channel_multiplier=1).then_inc(s_id, 1)
            for e in range(E):
                nc.gpsimd.memset(iota_e[:, e:e + 1], float(e)).then_inc(s_id, 1)
            with pool.Fori(0, C) as c:
                pool.wait_ge(s_zT, c + (C + 1))
                nc.gpsimd.tensor_copy(h0[:, bass.ds(c * BC, BC), :],
                                      zT[:, :].rearrange("p (b t) -> p b t", b=BC)).then_inc(s_zs, 1)

        @block.scalar
        def _(act):
            for dst, src in ((ffn_s, ffn_wT), (gnn_s, gnn_w), (gate_s, gate_wT), (b1_s, b1T), (b2_s, b2),
                             (w1_s, w1T)):
                act.dma_start(dst[:, :], src).then_inc(s_par, 16)
            for dst, src in ((ffnb_row, ffn_b), (gnnb_row, gnn_b), (gateb_row, gate_b)):
                act.dma_start(dst[:, :], src.partition_broadcast(P)).then_inc(s_par, 16)
            act.dma_start(w2_s[:, :, :], w2T).then_inc(s_par, 16)

            act.preload_act_table_set("natural_log_exp_and_others")

            def copy_half(n):
                act.wait_ge(s_grp, n * G + G // 2)
                act.wait_ge(s_t1, n)
                nc.scalar.copy(aggT[:, :], acc[0][:, :]).then_inc(s_half, 1)

            act.wait_ge(s_grp, G // 2)
            nc.scalar.copy(aggT[:, :], acc[0][:, :]).then_inc(s_half, 1)
            with act.Fori(1, C) as c:
                copy_half(c)

            steps = sum(1 if g in DVE_RECIP else 3 for g in range(G))

            def gate_exp(c):
                act.wait_ge(s_gap, c + 1)
                nc.scalar.activation(eg[:, :], gap[:, :], ACT.Exp).then_inc(s_eg, 1)

            def weights(c, gate):
                done = 0

                def chained(ins):
                    nonlocal done
                    done += 1
                    ins.then_inc(s_act, 1)
                    act.wait_ge(s_act, c * steps + done)

                for g in range(G):
                    slot = ring[:, g, :]
                    if g in DVE_RECIP:
                        act.wait_ge(s_rec, c * len(DVE_RECIP) + (DVE_RECIP.index(g) + 1))
                    else:
                        act.wait_ge(s_mask, c * G + (g + 1))
                        chained(nc.scalar.activation(slot, slot, ACT.Ln, bias=TINY))
                        chained(nc.scalar.activation(slot, slot, ACT.Exp, scale=-1.0))
                    chained(nc.scalar.activation(slot, slot, ACT.Square, bias=-1.0))
                    nc.scalar.activation(slot, slot, ACT.Exp, scale=-2.0).then_inc(s_wr, 1)
                    if g == 5:
                        copy_half(c + C)
                    if g == 6 and gate:
                        gate_exp(c - 1)
                assert done == steps

            weights(0, False)
            with act.Fori(1, C) as c:
                weights(c, True)
            gate_exp(C - 1)

            with act.Fori(0, C) as c:
                for e in range(E):
                    for k in range(0, K, 2):
                        n = e * K + k
                        act.wait_ge(s_hp, c * (E * K) + (n + 1))
                        nc.scalar.activation(hid[:, ((e % 2) * K + k) * T:((e % 2) * K + k + 1) * T], pH[0][:, :],
                                             ACT.Relu, bias=b1_s[:, n:n + 1]).then_inc(s_hd, 1)

        @block.vector
        def _(dve):
            def link(ins):
                dve.drain()

            def layer_norm(src, dst):
                for b in range(BC):
                    last = nc.vector.bn_stats(stats[:, b, :], src[:, b, :])
                link(last)
                for b in range(BC):
                    last = nc.vector.bn_aggr(mv[:, b, :], stats[:, b, :])
                link(last)
                nc.vector.tensor_scalar(hv[:, :], mv[:, :, 1], EPS, -0.5, ALU.add, ALU.mult)
                link(nc.vector.tensor_scalar(va[:, :], mv[:, :, 1], EPS, None, ALU.add))
                link(nc.vector.tensor_scalar(ya[:, :].bitcast(i32), va[:, :].bitcast(i32), 1, None,
                                             ALU.logical_shift_right))
                link(nc.vector.tensor_scalar(yb[:, :].bitcast(i32), ya[:, :].bitcast(i32), -1.0, MAGIC,
                                             ALU.mult, ALU.add))
                for _ in range(4):
                    link(nc.vector.tensor_tensor(out=ya[:, :], in0=yb[:, :], in1=yb[:, :], op=ALU.mult))
                    link(nc.vector.tensor_tensor(out=ya[:, :], in0=ya[:, :], in1=hv[:, :], op=ALU.mult))
                    link(nc.vector.scalar_tensor_tensor(out=yb[:, :], in0=ya[:, :], scalar=1.5, in1=yb[:, :],
                                                        op0=ALU.add, op1=ALU.mult))
                for b in range(BC):
                    last = nc.vector.tensor_scalar(dst[:, b, :], src[:, b, :], mv[:, b, 0:1], yb[:, b:b + 1],
                                                   ALU.subtract, ALU.mult)
                return last

            def rows(row):
                return row[:, :].unsqueeze(1).to_broadcast([P, BC, row.shape[1]])

            dve.wait_ge(s_x, 32)
            pv = pF[:, :].rearrange("p (b d) -> p b d", b=BC)
            tv = pT[:, :].rearrange("p (b d) -> p b d", b=BC)
            with dve.Fori(0, C) as c:
                link(layer_norm(xs[:, bass.ds(c * BC, BC), :], z))
                nc.vector.tensor_tensor(out=h0[:, bass.ds(c * BC, BC), :], in0=z[:, :, :], in1=rows(w_row),
                                        op=ALU.mult).then_inc(s_h0, 1)
            dve.wait_ge(s_par, 160)

            def finish_agg(n):
                dve.wait_ge(s_half, n + 1)
                dve.wait_ge(s_grp, (n + 1) * G)
                nc.vector.tensor_tensor(out=aggT[:, :], in0=acc[1][:, :], in1=aggT[:, :],
                                        op=ALU.add).then_inc(s_agg, 1)

            def add_agg(n, c):
                xc = xs[:, bass.ds(c * BC, BC), :]
                dve.wait_ge(s_t1, n + 1)
                link(nc.vector.tensor_tensor(out=xc, in0=tv, in1=xc, op=ALU.add))
                layer_norm(xc, z).then_inc(s_z1, 1)

            def copy_zT(s_from, s_to, n):
                dve.wait_ge(s_from, n + 1)
                nc.vector.tensor_copy(zT[:, :], pT[:, :]).then_inc(s_to, 1)

            def post0_a(c):
                finish_agg(c)
                add_agg(c, c)

            def post0_b(c):
                xc = xs[:, bass.ds(c * BC, BC), :]
                copy_zT(s_t2, s_zT, c)
                link(nc.vector.tensor_tensor(out=xc, in0=xc, in1=rows(ffnb_row), op=ALU.add))
                dve.wait_ge(s_f, c + 1)
                link(nc.vector.tensor_tensor(out=xc, in0=pv, in1=xc, op=ALU.add))
                layer_norm(xc, z).then_inc(s_z2, 1)

            def post0_c(c):
                copy_zT(s_t3, s_zT2, c)
                dve.wait_ge(s_m, c + 1)
                nc.vector.tensor_tensor(out=msg[:, bass.ds(c * BC, BC), :], in0=pv, in1=rows(gnnb_row),
                                        op=ALU.add).then_inc(s_msg, 1)

            with dve.Fori(0, C - 1) as c:
                post0_a(c)
                post0_b(c)
                post0_c(c)

            def mask(n, g):
                dve.wait_ge(s_in[g], 16 * (n + (C + 1)))
                nc.vector.scalar_tensor_tensor(out=ring[:, g, :], in0=ring[:, g, :], scalar=1.0,
                                               in1=ring[:, g, :], op0=ALU.is_lt,
                                               op1=ALU.mult).then_inc(s_mask, 1)
                if g in DVE_RECIP:
                    dve.wait_ge(s_mask, n * G + (g + 1))
                    link(nc.vector.tensor_scalar(ring[:, g, :], ring[:, g, :], TINY, None, ALU.max))
                    nc.vector.reciprocal(ring[:, g, :], ring[:, g, :]).then_inc(s_rec, 1)

            def gates_a(c):
                dve.wait_ge(s_gt, c + 1)
                gv = pF[:, 0:BC * E].rearrange("p (b e) -> p b e", b=BC)
                link(nc.vector.tensor_tensor(out=sc[:, :, :], in0=gv, in1=rows(gateb_row), op=ALU.add))
                for b in range(BC):
                    last = nc.vector.max(top[:, b, :], sc[:, b, :])
                link(last)
                for b in range(BC):
                    last = nc.vector.max_index(topi[:, b, :], top[:, b, :], sc[:, b, :])
                link(last)
                nc.vector.tensor_tensor(out=gap[:, :], in0=top[:, :, 1], in1=top[:, :, 0],
                                        op=ALU.subtract).then_inc(s_gap, 1)
                link(nc.vector.tensor_copy(topf[:, :, :], topi[:, :, 0:2]))

            def gates_b(c):
                dve.wait_ge(s_eg, c + 1)
                link(nc.vector.tensor_scalar(den[:, :], eg[:, :], 1.0, None, ALU.add))
                link(nc.vector.reciprocal(pr[:, :, 0], den[:, :]))
                link(nc.vector.tensor_tensor(out=pr[:, :, 1], in0=eg[:, :], in1=pr[:, :, 0], op=ALU.mult))
                for b in range(BC):
                    for k in range(2):
                        last = nc.vector.tensor_scalar(cj[:, k, :], iota_e[:, :], topf[:, b, k:k + 1],
                                                       pr[:, b, k:k + 1], ALU.is_equal, ALU.mult)
                    link(last)
                    last = nc.vector.tensor_tensor(out=comb[:, bass.ds(c * BC + b, 1), :].rearrange("p a e -> p (a e)"),
                                                   in0=cj[:, 0, :], in1=cj[:, 1, :], op=ALU.add)
                    last.then_inc(s_comb, 1)
                    dve.wait_ge(s_comb, c * BC + (b + 1))

            for g in range(3):
                mask(0, g)
            post0_a(C - 1)
            mask(0, 3)
            post0_b(C - 1)
            for g in range(4, G - 1):
                mask(0, g)
            post0_c(C - 1)
            mask(0, G - 1)
            dve.wait_ge(s_id, 2 + E)
            with dve.Fori(1, C) as c:
                for g in range(3):
                    mask(c, g)
                finish_agg(c + (C - 1))
                mask(c, 3)
                add_agg(c + (C - 1), c - 1)
                mask(c, 4)
                dve.wait_ge(s_zs, c - 1)
                copy_zT(s_t2, s_zT, c + (C - 1))
                mask(c, 5)
                gates_a(c - 1)
                mask(c, 6)
                mask(c, 7)
                gates_b(c - 1)
            finish_agg(2 * C - 1)
            add_agg(2 * C - 1, C - 1)
            dve.wait_ge(s_zs, C - 1)
            copy_zT(s_t2, s_zT, 2 * C - 1)
            gates_a(C - 1)
            gates_b(C - 1)

            def hidden(c, e):
                for k in range(1, K, 2):
                    n = e * K + k
                    dve.wait_ge(s_hp, c * (E * K) + (n + 1))
                    nc.vector.tensor_scalar(hid[:, ((e % 2) * K + k) * T:((e % 2) * K + k + 1) * T], pH[1][:, :],
                                            b1_s[:, n:n + 1], 0.0, ALU.add, ALU.max).then_inc(s_hd2, 1)

            with dve.Fori(0, C) as c:
                nc.vector.tensor_copy(comb_c[:, :, :], comb[:, bass.ds(c * BC, BC), :]).then_inc(s_cc, 1)
                dve.wait_ge(s_ct, c + 1)
                nc.vector.tensor_copy(combT[:, :, :], pT[0:E, :].rearrange("p (b t) -> p b t", b=BC)).then_inc(s_cT, 1)
                xc = xs[:, bass.ds(c * BC, BC), :]
                dve.wait_ge(s_f, c + (C + 1))
                nc.vector.tensor_tensor(out=xc, in0=pv, in1=xc, op=ALU.add).then_inc(s_ya, 1)
                hidden(c, 0)
                for e in range(E):
                    if e + 1 < E:
                        hidden(c, e + 1)
                    dve.wait_ge(s_y, c * E + (e + 1))
                    dve.wait_ge(s_ya, c * (E + 1) + (e + 1))
                    for b in range(BC):
                        xb = xs[:, bass.ds(c * BC + b, 1), :].rearrange("p a d -> p (a d)")
                        last = nc.vector.scalar_tensor_tensor(
                            out=xb, in0=pY[e % 2][:, b * D:(b + 1) * D],
                            scalar=comb[:, bass.ds(c * BC + b, 1), e:e + 1].rearrange("p a e -> p (a e)"),
                            in1=xb, op0=ALU.mult, op1=ALU.add)
                    last.then_inc(s_ya, 1)

        @block.tensor
        def _(pe):
            def group(n, g, feats, ready):
                ready()
                half = g * 2 // G
                if g * 2 % G == 0:
                    free = (s_half, s_agg)[half]
                    if isinstance(n, int):
                        if n:
                            pe.wait_ge(free, n)
                    else:
                        pe.wait_ge(free, n)
                for jj in range(J):
                    j = g * J + jj
                    last = nc.tensor.matmul(acc[half][:, :], feats[:, j, :], ring[:, g, jj * T:(jj + 1) * T],
                                            start=(j % (NB // 2) == 0), stop=(j % (NB // 2) == NB // 2 - 1))
                last.then_inc(s_grp, 1)

            def transposes(src, done):
                for b in range(BC):
                    last = nc.tensor.transpose(pT[:, b * P:(b + 1) * P], src(b), ident[:, :])
                last.then_inc(done, 1)

            def products(w, width, done):
                for b in range(BC):
                    last = nc.tensor.matmul(pF[:, b * width:(b + 1) * width], zT[:, b * P:(b + 1) * P], w,
                                            start=True, stop=True)
                last.then_inc(done, 1)

            def t1(n):
                pe.wait_ge(s_agg, n + 1)
                transposes(lambda b: aggT[:, b * P:(b + 1) * P], s_t1)

            def t2(n):
                pe.wait_ge(s_z1, n + 1)
                transposes(lambda b: z[:, b, :], s_t2)

            def ffn(n):
                pe.wait_ge(s_zT, n + 1)
                products(ffn_s[:, :], D, s_f)

            def t3(n):
                pe.wait_ge(s_z2, n + 1)
                transposes(lambda b: z[:, b, :], s_t3)

            def messages(n):
                pe.wait_ge(s_zT2, n + 1)
                products(gnn_s[:, :], D, s_m)

            def gates(n):
                pe.wait_ge(s_zT, n + 1)
                products(gate_s[:, :], E, s_gt)

            pe.wait_ge(s_id, 2)
            for g in range(G):
                def ready():
                    pe.wait_ge(s_in[g], 16)
                    pe.wait_ge(s_h0, g + 1)
                group(0, g, h0, ready)
            pe.wait_ge(s_par, 160)

            STEPS0 = {0: t1, 2: t2, 3: ffn, 5: t3, 6: messages}
            STEPS1 = {0: t1, 2: t2, 3: gates}
            with pe.Fori(1, C) as c:
                for g in range(G):
                    group(c, g, h0, lambda: pe.wait_ge(s_in[g], (c + 1) * 16))
                    if g in STEPS0:
                        STEPS0[g](c - 1)
            for g in range(G):
                def ready():
                    pe.wait_ge(s_wr, g + 1)
                    pe.wait_ge(s_msg, g + 1)
                group(C, g, msg, ready)
                if g in STEPS0:
                    STEPS0[g](C - 1)
            with pe.Fori(1, C) as c:
                for g in range(G):
                    group(c + C, g, msg, lambda: pe.wait_ge(s_wr, c * G + (g + 1)))
                    if g in STEPS1:
                        STEPS1[g](c + (C - 1))
            for g in STEPS1:
                STEPS1[g](2 * C - 1)

            pe.wait_ge(s_comb, NB)
            pe.wait_ge(s_zs, C)
            with pe.Fori(0, C) as c:
                pe.wait_ge(s_cc, c + 1)
                for b in range(BC):
                    last = nc.tensor.transpose(pT[0:E, b * P:(b + 1) * P],
                                               comb_c[:, b, :], ident[:, :])
                last.then_inc(s_ct, 1)
                pe.wait_ge(s_cT, c + 1)
                for b in range(BC):
                    last = nc.tensor.matmul(pF[:, b * D:(b + 1) * D], combT[:, b, :], b2_s[:, :], start=True, stop=True)
                last.then_inc(s_f, 1)

                def up(e):
                    for k in range(K):
                        n = e * K + k
                        pe.wait_ge((s_hd, s_hd2)[k % 2], c * (E * K // 2) + n // 2)
                        nc.tensor.matmul(pH[k % 2][:, :], w1_s[:, n * P:(n + 1) * P],
                                         h0[:, bass.ds(c * BC, BC), :],
                                         start=True, stop=True).then_inc(s_hp, 1)

                def down(e):
                    pe.wait_ge(s_hd, c * (E * K // 2) + (e + 1) * K // 2)
                    pe.wait_ge(s_hd2, c * (E * K // 2) + (e + 1) * K // 2)
                    pe.wait_ge(s_ya, c * (E + 1) + e)
                    for b in range(BC):
                        for k in range(K):
                            o = ((e % 2) * K + k) * T + b * P
                            last = nc.tensor.matmul(pY[e % 2][:, b * D:(b + 1) * D], hid[:, o:o + P],
                                                    w2_s[:, e * K + k, :], start=(k == 0), stop=(k == K - 1))
                    last.then_inc(s_y, 1)

                up(0)
                for e in range(E):
                    if e + 1 < E:
                        up(e + 1)
                    down(e)


def kernel(**inputs):
    import numpy as _np
    import concourse.bacc as _bacc
    from concourse import mybir as _mybir
    from concourse.bass_utils import run_bass_kernel_spmd as _run

    P, T, J = 128, 512, 4
    a = {k: _np.asarray(v) for k, v in inputs.items()}
    n, d = a["x"].shape
    e, h = a["L1_ffn_b1"].shape
    laid = {
        "x": a["x"],
        "adjT": a["adj"].reshape(n // T, T, n // (J * P), J, P).transpose(0, 2, 4, 3, 1).reshape(n // T, n // (J * P), P, J * T),
        "w_l0": a["L0_gnn_W"],
        "ffn_wT": a["L0_ffn_weight"].T,
        "ffn_b": a["L0_ffn_bias"],
        "gnn_w": a["L1_gnn_W"],
        "gnn_b": a["L1_gnn_B"],
        "gate_wT": a["L1_ffn_Wg"].T,
        "gate_b": a["L1_ffn_bg"],
        "w1T": a["L1_ffn_W1"].reshape(e * h, d).T,
        "b1T": a["L1_ffn_b1"].reshape(e * h // P, P).T,
        "w2T": a["L1_ffn_W2"].reshape(e, d, h // P, P).transpose(3, 0, 2, 1).reshape(P, e * h // P, d),
        "b2": a["L1_ffn_b2"],
    }
    nc = _bacc.Bacc("TRN2", target_bir_lowering=False, num_devices=1)
    arrays, args = {}, []
    for name, v in laid.items():
        v = _np.ascontiguousarray(v)
        arrays[f"in_{name}"] = v
        args.append(nc.dram_tensor(f"in_{name}", v.shape, _mybir.dt.from_np(v.dtype), kind="ExternalInput").ap())
    out = nc.dram_tensor("out_0", (n, d), _mybir.dt.from_np(a["x"].dtype), kind="ExternalOutput").ap()
    gnn_ffn_gnn_moe_kernel(nc, *args, out)
    r = _run(nc, [arrays], core_ids=[0])
    return r.results[0]["out_0"]
```

```python
import concourse.bass as bass
from concourse import mybir
from contextlib import ExitStack


def gnn_ffn_gnn_moe_kernel(
    nc: bass.Bass,
    x: bass.AP,
    adjT: bass.AP,
    w_l0: bass.AP,
    ffn_wT: bass.AP,
    ffn_b: bass.AP,
    gnn_w: bass.AP,
    gnn_b: bass.AP,
    gate_wT: bass.AP,
    gate_b: bass.AP,
    experts: bass.AP,
    b2: bass.AP,
    out: bass.AP,
):
    f32 = mybir.dt.float32
    i32 = mybir.dt.int32
    u32 = mybir.dt.uint32
    ALU = mybir.AluOpType
    ACT = mybir.ActivationFunctionType
    AX = mybir.AxisListType

    P = 128
    D = x.shape[1]
    N = x.shape[0]
    NB = N // P
    C, G = adjT.shape[0], adjT.shape[1]
    T = N // C
    BC = T // P
    J = NB // G
    GT = J * T
    E = gate_b.shape[0]
    K = experts.shape[2] // (P + D + 1)
    S = 2
    TS = S * P
    MT = 2 * N // TS + E - 1
    REGION = N + TS
    DUMMY = MT - 2 * N // TS
    RW = D + 2
    SLOTS = 4
    EPS = 1e-5
    TINY = 2.0 ** -60
    MAGIC = float(0x5F3759DF)
    DVE_RECIP = (2,)

    ctx = ExitStack()
    with ctx:
        def sb(name, shape, dt=f32):
            return ctx.enter_context(nc.sbuf_tensor(name, shape, dt))

        def pb(name):
            return ctx.enter_context(nc.psum_tensor(name, [P, 512], f32))

        def sem(name):
            return ctx.enter_context(nc.semaphore(name))

        xs = sb("xs", [P, NB, D])
        h0 = sb("h0", [P, NB, D])
        msg = sb("msg", [P, NB, D])
        ring = sb("ring", [P, G, GT])
        ffn_s = sb("ffn_s", [P, D])
        gnn_s = sb("gnn_s", [P, D])
        gate_s = sb("gate_s", [P, E])
        w_row = sb("w_row", [P, D])
        ffnb_row = sb("ffnb_row", [P, D])
        gnnb_row = sb("gnnb_row", [P, D])
        gateb_row = sb("gateb_row", [P, E])
        ident = sb("ident", [P, P])
        before = sb("before", [P, P])
        ones = sb("ones", [P, P])
        iota_e = sb("iota_e", [P, E])
        region_e = sb("region_e", [P, E])
        out_row = sb("out_row", [P, 2, BC], i32)
        first_row = sb("first_row", [P, 2, BC], i32)
        step_row = sb("step_row", [P, 2, BC], i32)
        count_t = sb("count_t", [1, N // TS])
        iota_m = sb("iota_m", [1, MT])
        row_m = sb("row_m", [1, MT])
        padding = sb("padding", [P, S, RW])
        aggT = sb("aggT", [P, T])
        z = sb("z", [P, BC, D])
        zT = sb("zT", [P, T])
        stats = sb("stats", [P, BC, 6])
        mv = sb("mv", [P, BC, 2])
        va = sb("va", [P, BC])
        hv = sb("hv", [P, BC])
        ya = sb("ya", [P, BC])
        yb = sb("yb", [P, BC])
        sc = sb("sc", [P, BC, E])
        top = sb("top", [P, BC, 8])
        topi = sb("topi", [P, BC, 8], u32)
        topf = sb("topf", [P, BC, 2])
        gap = sb("gap", [P, BC])
        eg = sb("eg", [P, BC])
        den = sb("den", [P, BC])
        rows3 = sb("rows3", [P, 2, BC, RW])
        sel = sb("sel", [P, 2, BC, E])
        both = sb("both", [P, BC + 1, E])
        rank = sb("rank", [P, BC + 1, E])
        seen = sb("seen", [P, E])
        prow = sb("prow", [P, BC, E])
        posf = sb("posf", [P, 2, BC])
        posu = sb("posu", [P, 2, BC], u32)
        has_t = sb("has_t", [1, E, N // TS])
        tiles_e = sb("tiles_e", [1, E])
        ends_e = sb("ends_e", [1, E])
        one_e = sb("one_e", [1, E])
        skip_e = sb("skip_e", [1, E])
        past = sb("past", [1, MT, E])
        skipped = sb("skipped", [1, MT, E])
        tab_f = sb("tab_f", [1, 2, MT])
        table = sb("table", [1, 2, MT], i32)
        pad_f = sb("pad_f", [1, E])
        pad_at = sb("pad_at", [1, E], i32)
        srt = sb("srt", [P, SLOTS, S, RW])
        wts = sb("wts", [P, SLOTS, K * (P + D + 1)])
        b2_t = sb("b2_t", [P, SLOTS, D])
        zsT = sb("zsT", [P, 2, TS])
        hid = sb("hid", [P, 2, K, TS])
        yb2 = sb("yb2", [P, SLOTS, S, D])
        ysc = sb("ysc", [P, SLOTS, S, D])
        pick_in = ring[:, :, :].rearrange("p g n -> p (g n)")

        sorted_rows = nc.dram_tensor("sorted_rows", [E * REGION + DUMMY * TS, RW], f32).ap()
        picked = nc.dram_tensor("picked", [2 * N, D], f32).ap()

        acc = [pb("accA"), pb("accB")]
        pT = pb("pT")
        pF = pb("pF")
        pR = pb("pR")
        pH = pb("pH")
        pY = [pb("pY0"), pb("pY1")]
        pHid = [acc, [pR, pH]]
        pZ = [pT, pF]

        s_x = sem("s_x")
        s_par = sem("s_par")
        s_in = [sem(f"s_in{g}") for g in range(G)]
        s_id = sem("s_id")
        s_h0 = sem("s_h0")
        s_grp = sem("s_grp")
        s_half = sem("s_half")
        s_agg = sem("s_agg")
        s_t1 = sem("s_t1")
        s_z1 = sem("s_z1")
        s_t2 = sem("s_t2")
        s_zT = sem("s_zT")
        s_f = sem("s_f")
        s_z2 = sem("s_z2")
        s_t3 = sem("s_t3")
        s_zT2 = sem("s_zT2")
        s_m = sem("s_m")
        s_msg = sem("s_msg")
        s_mask = sem("s_mask")
        s_rec = sem("s_rec")
        s_act = sem("s_act")
        s_wr = sem("s_wr")
        s_gt = sem("s_gt")
        s_gap = sem("s_gap")
        s_eg = sem("s_eg")
        s_cst = sem("s_cst")
        s_pad0 = sem("s_pad0")
        s_sel = sem("s_sel")
        s_rk = sem("s_rk")
        s_pos = sem("s_pos")
        s_sc = sem("s_sc")
        s_tab = sem("s_tab")
        s_pad = sem("s_pad")
        s_srt = [sem(f"s_srt{i}") for i in range(SLOTS)]
        s_wt = [sem(f"s_wt{i}") for i in range(SLOTS)]
        s_tr = sem("s_tr")
        s_zc = sem("s_zc")
        s_up = sem("s_up")
        s_ha = sem("s_ha")
        s_hd = sem("s_hd")
        s_dn = sem("s_dn")
        s_yb = sem("s_yb")
        s_ysc = [sem(f"s_ysc{i}") for i in range(SLOTS)]
        s_pk = [sem(f"s_pk{c}") for c in range(C)]
        s_fin = sem("s_fin")
        s_out = sem("s_out")

        CST = 15
        MAIN = (MT - 2) // SLOTS

        block = ctx.enter_context(nc.Block())

        def at(m):
            return slice(m, m + 1) if isinstance(m, int) else bass.ds(m, 1)

        def pad(eng, e):
            row = eng.value_load(pad_at[0:1, e:e + 1], min_val=0, max_val=E * REGION - TS)
            eng.dma_start(sorted_rows[bass.ds(row, TS), :].rearrange("(p s) d -> p s d", s=S),
                          padding[:, :, :]).then_inc(s_pad, 16)

        @block.sync
        def _(sp):
            sp.dma_start(xs[:, :, :], x.rearrange("(b p) d -> p b d", p=P)).then_inc(s_x, 16)
            sp.dma_start(w_row[:, :], w_l0.partition_broadcast(P)).then_inc(s_x, 16)
            for g in range(G):
                sp.dma_start(ring[:, g, :], adjT[0, g]).then_inc(s_in[g], 16)
            for half in range(2):
                with sp.Fori(1 - half, C) as c:
                    for g in range(G):
                        sp.wait_ge(s_grp, (c + (half * C - 1)) * G + (g + 1))
                        sp.dma_start(ring[:, g, :], adjT[c, g]).then_inc(s_in[g], 16)

            sp.wait_ge(s_sc, 16 * 2 * NB)
            sp.wait_ge(s_tab, 2)
            for e in range(0, E, 2):
                pad(sp, e)

            def load_tile(m, slot, turn):
                first = sp.value_load(table[0:1, 0:1, at(m)], min_val=0, max_val=E * REGION + (DUMMY - 1) * TS)
                expert = sp.value_load(table[0:1, 1:2, at(m)], min_val=0, max_val=E - 1)
                if turn is not None:
                    sp.wait_ge(s_dn, m - (SLOTS - 1))
                    sp.wait_ge(s_yb, m - (SLOTS - 1))
                sp.dma_start(wts[:, slot, :], experts[bass.ds(expert, 1), :, :].rearrange("a p n -> (a p) n")
                             ).then_inc(s_wt[slot], 16)
                sp.dma_start(b2_t[:, slot, :], b2[bass.ds(expert, 1), :].rearrange("a d -> (a d)")
                             .partition_broadcast(P)).then_inc(s_wt[slot], 16)
                if turn is not None:
                    sp.wait_ge(s_ysc[slot], turn * (16 * S))
                elif slot == 0:
                    sp.wait_ge(s_pad, 16 * E)
                    sp.wait_ge(s_pad0, 16 * DUMMY)
                sp.dma_start(srt[:, slot, :, :], sorted_rows[bass.ds(first, TS), :].rearrange("(p s) d -> p s d", s=S)
                             ).then_inc(s_srt[slot], 16)

            for m in range(SLOTS):
                load_tile(m, m, None)
            with sp.Fori(1, MT // SLOTS) as i:
                for u in range(SLOTS):
                    load_tile(i * SLOTS + u, u, i)
            for m in range(MT // SLOTS * SLOTS, MT):
                load_tile(m, m % SLOTS, m // SLOTS)

            for i in range(SLOTS):
                sp.wait_ge(s_ysc[i], 16 * S * ((MT - i + SLOTS - 1) // SLOTS))
            for c in range(C):
                for k in range(2):
                    sp.dma_start(pick_in[:, (c * 2 + k) * BC * D:(c * 2 + k + 1) * BC * D]
                                 .rearrange("p (b d) -> p b d", b=BC),
                                 picked[k * N + c * T:k * N + (c + 1) * T, :].rearrange("(b p) d -> p b d", p=P)
                                 ).then_inc(s_pk[c], 16)
            for c in range(C):
                sp.wait_ge(s_fin, c + 1)
                sp.dma_start(out[c * T:(c + 1) * T, :].rearrange("(b p) d -> p b d", p=P),
                             xs[:, c * BC:(c + 1) * BC, :]).then_inc(s_out, 16)
            sp.wait_ge(s_out, 16 * C)

        @block.gpsimd
        def _(pool):
            nc.gpsimd.memset(ident[:, :], 0.0).then_inc(s_id, 1)
            pool.wait_ge(s_id, 1)
            nc.gpsimd.affine_select(out=ident[:, :], in_=ident[:, :], compare_op=ALU.not_equal, fill=1.0,
                                    base=0, pattern=[[-1, P]], channel_multiplier=1).then_inc(s_id, 1)
            nc.gpsimd.memset(ones[:, :], 1.0).then_inc(s_cst, 1)
            pool.wait_ge(s_cst, 1)
            nc.gpsimd.affine_select(out=before[:, :], in_=ones[:, :], compare_op=ALU.is_gt, fill=0.0,
                                    base=0, pattern=[[1, P]], channel_multiplier=-1).then_inc(s_cst, 1)
            for dst, pattern, channel in ((iota_e[:, :], [[1, E]], 0), (region_e[:, :], [[REGION, E]], 0),
                                          (out_row[:, :, :], [[N, 2], [P, BC]], 1),
                                          (count_t[:, :], [[TS, N // TS]], 0), (iota_m[:, :], [[1, MT]], 0),
                                          (row_m[:, :], [[TS, MT]], 0)):
                nc.gpsimd.iota(dst, pattern=pattern, base=0, channel_multiplier=channel,
                               allow_small_or_imprecise_dtypes=True).then_inc(s_cst, 1)
            for dst, value in ((both[:, :, :], 0.0), (seen[:, :], 0.0), (one_e[:, :], 1.0),
                               (padding[:, :, 0:D + 1], 0.0)):
                nc.gpsimd.memset(dst, value).then_inc(s_cst, 1)
            nc.gpsimd.memset(padding[:, :, D + 1:RW].bitcast(i32), 2 * N).then_inc(s_cst, 1)
            nc.gpsimd.memset(first_row[:, :, :], 0).then_inc(s_cst, 1)
            nc.gpsimd.memset(step_row[:, :, :], T).then_inc(s_cst, 1)
            pool.wait_ge(s_cst, CST)

            with pool.Fori(0, C) as c:
                pool.wait_ge(s_pos, c + 1)
                nc.gpsimd.tensor_tensor(out=rows3[:, :, :, D + 1].bitcast(i32), in0=out_row[:, :, :],
                                        in1=first_row[:, :, :], op=ALU.add)
                pool.drain()
                nc.gpsimd.tensor_tensor(out=first_row[:, :, :], in0=first_row[:, :, :], in1=step_row[:, :, :],
                                        op=ALU.add)
                pool.drain()
                for k in range(2):
                    for b in range(BC):
                        nc.gpsimd.indirect_dma_start(
                            out=sorted_rows, out_offset=bass.IndirectOffsetOnAxis(ap=posu[:, k, b:b + 1], axis=0),
                            in_=rows3[:, k, b, :], in_offset=None).then_inc(s_sc, 16)

            def store_tile(m, slot):
                pool.wait_ge(s_yb, m + 1)
                nc.gpsimd.tensor_tensor(out=ysc[:, slot, :, :], in0=yb2[:, slot, :, :],
                                        in1=srt[:, slot, :, D:D + 1].to_broadcast([P, S, D]), op=ALU.mult)
                pool.drain()
                for s in range(S):
                    nc.gpsimd.indirect_dma_start(
                        out=picked,
                        out_offset=bass.IndirectOffsetOnAxis(ap=srt[:, slot, s, D + 1:RW].bitcast(u32), axis=0),
                        in_=ysc[:, slot, s, :], in_offset=None, bounds_check=2 * N - 1,
                        oob_is_err=False).then_inc(s_ysc[slot], 16)

            with pool.Fori(0, MT // SLOTS) as i:
                for u in range(SLOTS):
                    store_tile(i * SLOTS + u, u)
            for m in range(MT // SLOTS * SLOTS, MT):
                store_tile(m, m % SLOTS)

        @block.scalar
        def _(act):
            for dst, src in ((ffn_s, ffn_wT), (gnn_s, gnn_w), (gate_s, gate_wT)):
                act.dma_start(dst[:, :], src).then_inc(s_par, 16)
            for dst, src in ((ffnb_row, ffn_b), (gnnb_row, gnn_b), (gateb_row, gate_b)):
                act.dma_start(dst[:, :], src.partition_broadcast(P)).then_inc(s_par, 16)
            act.wait_ge(s_cst, CST)
            for i in range(DUMMY):
                row = E * REGION + i * TS
                act.dma_start(sorted_rows[row:row + TS, :].rearrange("(p s) d -> p s d", s=S),
                              padding[:, :, :]).then_inc(s_pad0, 16)
            act.preload_act_table_set("natural_log_exp_and_others")

            def copy_half(n):
                act.wait_ge(s_grp, n * G + G // 2)
                act.wait_ge(s_t1, n)
                nc.scalar.copy(aggT[:, :], acc[0][:, :]).then_inc(s_half, 1)

            act.wait_ge(s_grp, G // 2)
            nc.scalar.copy(aggT[:, :], acc[0][:, :]).then_inc(s_half, 1)
            with act.Fori(1, C) as c:
                copy_half(c)

            steps = sum(1 if g in DVE_RECIP else 3 for g in range(G))

            def gate_exp(c):
                act.wait_ge(s_gap, c + 1)
                nc.scalar.activation(eg[:, :], gap[:, :], ACT.Exp).then_inc(s_eg, 1)

            def weights(c, gate):
                done = 0

                def chained(ins):
                    nonlocal done
                    done += 1
                    ins.then_inc(s_act, 1)
                    act.wait_ge(s_act, c * steps + done)

                for g in range(G):
                    slot = ring[:, g, :]
                    if g in DVE_RECIP:
                        act.wait_ge(s_rec, c * len(DVE_RECIP) + (DVE_RECIP.index(g) + 1))
                    else:
                        act.wait_ge(s_mask, c * G + (g + 1))
                        chained(nc.scalar.activation(slot, slot, ACT.Ln, bias=TINY))
                        chained(nc.scalar.activation(slot, slot, ACT.Exp, scale=-1.0))
                    chained(nc.scalar.activation(slot, slot, ACT.Square, bias=-1.0))
                    nc.scalar.activation(slot, slot, ACT.Exp, scale=-2.0).then_inc(s_wr, 1)
                    if g == 5:
                        copy_half(c + C)
                    if g == 6 and gate:
                        gate_exp(c - 1)
                assert done == steps

            weights(0, False)
            with act.Fori(1, C) as c:
                weights(c, True)
            gate_exp(C - 1)

            act.wait_ge(s_sc, 16 * 2 * NB)
            act.wait_ge(s_tab, 2)
            for e in range(1, E, 2):
                pad(act, e)

            def relu(m, slot, par):
                act.wait_ge(s_up, 2 * m + 1)
                for k in range(K // 2):
                    last = nc.scalar.activation(hid[:, par, k, :], pHid[par][0][:, k * TS:(k + 1) * TS], ACT.Relu,
                                                bias=wts[:, slot, K * (P + D) + k:K * (P + D) + k + 1])
                last.then_inc(s_ha, 1)

            relu(0, 0, 0)
            with act.Fori(0, MAIN) as i:
                for u in range(SLOTS):
                    relu(i * SLOTS + (u + 1), (u + 1) % SLOTS, (u + 1) % 2)
            for m in range(MAIN * SLOTS + 1, MT):
                relu(m, m % SLOTS, m % 2)

        @block.vector
        def _(dve):
            def link(ins):
                dve.drain()

            def layer_norm(src, dst):
                for b in range(BC):
                    last = nc.vector.bn_stats(stats[:, b, :], src[:, b, :])
                link(last)
                for b in range(BC):
                    last = nc.vector.bn_aggr(mv[:, b, :], stats[:, b, :])
                link(last)
                nc.vector.tensor_scalar(hv[:, :], mv[:, :, 1], EPS, -0.5, ALU.add, ALU.mult)
                link(nc.vector.tensor_scalar(va[:, :], mv[:, :, 1], EPS, None, ALU.add))
                link(nc.vector.tensor_scalar(ya[:, :].bitcast(i32), va[:, :].bitcast(i32), 1, None,
                                             ALU.logical_shift_right))
                link(nc.vector.tensor_scalar(yb[:, :].bitcast(i32), ya[:, :].bitcast(i32), -1.0, MAGIC,
                                             ALU.mult, ALU.add))
                for _ in range(4):
                    link(nc.vector.tensor_tensor(out=ya[:, :], in0=yb[:, :], in1=yb[:, :], op=ALU.mult))
                    link(nc.vector.tensor_tensor(out=ya[:, :], in0=ya[:, :], in1=hv[:, :], op=ALU.mult))
                    link(nc.vector.scalar_tensor_tensor(out=yb[:, :], in0=ya[:, :], scalar=1.5, in1=yb[:, :],
                                                        op0=ALU.add, op1=ALU.mult))
                for b in range(BC):
                    last = nc.vector.tensor_scalar(dst[:, b, :], src[:, b, :], mv[:, b, 0:1], yb[:, b:b + 1],
                                                   ALU.subtract, ALU.mult)
                return last

            def rows(row):
                return row[:, :].unsqueeze(1).to_broadcast([P, BC, row.shape[1]])

            dve.wait_ge(s_x, 32)
            pv = pF[:, :].rearrange("p (b d) -> p b d", b=BC)
            tv = pT[:, :].rearrange("p (b d) -> p b d", b=BC)
            with dve.Fori(0, C) as c:
                link(layer_norm(xs[:, bass.ds(c * BC, BC), :], z))
                nc.vector.tensor_tensor(out=h0[:, bass.ds(c * BC, BC), :], in0=z[:, :, :], in1=rows(w_row),
                                        op=ALU.mult).then_inc(s_h0, 1)
            dve.wait_ge(s_par, 96)

            def finish_agg(n):
                dve.wait_ge(s_half, n + 1)
                dve.wait_ge(s_grp, (n + 1) * G)
                nc.vector.tensor_tensor(out=aggT[:, :], in0=acc[1][:, :], in1=aggT[:, :],
                                        op=ALU.add).then_inc(s_agg, 1)

            def add_agg(n, c, z=z):
                xc = xs[:, bass.ds(c * BC, BC), :]
                dve.wait_ge(s_t1, n + 1)
                link(nc.vector.tensor_tensor(out=xc, in0=tv, in1=xc, op=ALU.add))
                layer_norm(xc, z).then_inc(s_z1, 1)

            def copy_zT(s_from, s_to, n):
                dve.wait_ge(s_from, n + 1)
                nc.vector.tensor_copy(zT[:, :], pT[:, :]).then_inc(s_to, 1)

            def post0_a(c):
                finish_agg(c)
                add_agg(c, c)

            def post0_b(c):
                xc = xs[:, bass.ds(c * BC, BC), :]
                copy_zT(s_t2, s_zT, c)
                link(nc.vector.tensor_tensor(out=xc, in0=xc, in1=rows(ffnb_row), op=ALU.add))
                dve.wait_ge(s_f, c + 1)
                link(nc.vector.tensor_tensor(out=xc, in0=pv, in1=xc, op=ALU.add))
                layer_norm(xc, z).then_inc(s_z2, 1)

            def post0_c(c):
                copy_zT(s_t3, s_zT2, c)
                dve.wait_ge(s_m, c + 1)
                nc.vector.tensor_tensor(out=msg[:, bass.ds(c * BC, BC), :], in0=pv, in1=rows(gnnb_row),
                                        op=ALU.add).then_inc(s_msg, 1)

            with dve.Fori(0, C - 1) as c:
                post0_a(c)
                post0_b(c)
                post0_c(c)

            def mask(n, g):
                dve.wait_ge(s_in[g], 16 * (n + (C + 1)))
                nc.vector.scalar_tensor_tensor(out=ring[:, g, :], in0=ring[:, g, :], scalar=1.0,
                                               in1=ring[:, g, :], op0=ALU.is_lt,
                                               op1=ALU.mult).then_inc(s_mask, 1)
                if g in DVE_RECIP:
                    dve.wait_ge(s_mask, n * G + (g + 1))
                    link(nc.vector.tensor_scalar(ring[:, g, :], ring[:, g, :], TINY, None, ALU.max))
                    nc.vector.reciprocal(ring[:, g, :], ring[:, g, :]).then_inc(s_rec, 1)

            rows3z = rows3[:, 0, :, 0:D]

            def gates_a(c):
                dve.wait_ge(s_gt, c + 1)
                gv = pF[:, 0:BC * E].rearrange("p (b e) -> p b e", b=BC)
                link(nc.vector.tensor_tensor(out=sc[:, :, :], in0=gv, in1=rows(gateb_row), op=ALU.add))
                for b in range(BC):
                    last = nc.vector.max(top[:, b, :], sc[:, b, :])
                link(last)
                for b in range(BC):
                    last = nc.vector.max_index(topi[:, b, :], top[:, b, :], sc[:, b, :])
                link(last)
                nc.vector.tensor_tensor(out=gap[:, :], in0=top[:, :, 1], in1=top[:, :, 0],
                                        op=ALU.subtract).then_inc(s_gap, 1)
                link(nc.vector.tensor_copy(topf[:, :, :], topi[:, :, 0:2]))
                for k in range(2):
                    last = nc.vector.tensor_tensor(out=sel[:, k, :, :], in0=rows(iota_e),
                                                   in1=topf[:, :, k:k + 1].to_broadcast([P, BC, E]),
                                                   op=ALU.is_equal)
                link(last)
                nc.vector.tensor_tensor(out=both[:, 0:BC, :], in0=sel[:, 0, :, :], in1=sel[:, 1, :, :],
                                        op=ALU.add).then_inc(s_sel, 1)

            def gates_b(c):
                nc.vector.tensor_copy(rows3[:, 1, :, 0:D], rows3z)
                dve.wait_ge(s_eg, c + 1)
                link(nc.vector.tensor_scalar(den[:, :], eg[:, :], 1.0, None, ALU.add))
                link(nc.vector.reciprocal(rows3[:, 0, :, D], den[:, :]))
                nc.vector.tensor_tensor(out=rows3[:, 1, :, D], in0=eg[:, :], in1=rows3[:, 0, :, D], op=ALU.mult)
                dve.wait_ge(s_rk, c + 1)
                link(nc.vector.tensor_tensor(out=rank[:, :, :],
                                             in0=pR[:, 0:(BC + 1) * E].rearrange("p (b e) -> p b e", e=E),
                                             in1=seen[:, :].unsqueeze(1).to_broadcast([P, BC + 1, E]), op=ALU.add))
                link(nc.vector.tensor_tensor(out=rank[:, 0:BC, :], in0=rank[:, 0:BC, :], in1=rows(region_e),
                                             op=ALU.add))
                nc.vector.tensor_copy(seen[:, :], rank[:, BC, :])
                for k in range(2):
                    link(nc.vector.tensor_tensor(out=prow[:, :, :], in0=rank[:, 0:BC, :], in1=sel[:, k, :, :],
                                                 op=ALU.mult))
                    link(nc.vector.tensor_reduce(posf[:, k, :], prow[:, :, :], AX.X, ALU.add))
                nc.vector.tensor_copy(posu[:, :, :], posf[:, :, :]).then_inc(s_pos, 1)

            for g in range(3):
                mask(0, g)
            post0_a(C - 1)
            mask(0, 3)
            post0_b(C - 1)
            for g in range(4, G - 1):
                mask(0, g)
            post0_c(C - 1)
            mask(0, G - 1)
            dve.wait_ge(s_cst, CST)
            with dve.Fori(1, C) as c:
                for g in range(4):
                    mask(c, g)
                finish_agg(c + (C - 1))
                mask(c, 4)
                dve.wait_ge(s_sc, (c - 1) * (16 * 2 * BC))
                add_agg(c + (C - 1), c - 1, rows3z)
                mask(c, 5)
                copy_zT(s_t2, s_zT, c + (C - 1))
                mask(c, 6)
                gates_a(c - 1)
                mask(c, 7)
                gates_b(c - 1)
            finish_agg(2 * C - 1)
            dve.wait_ge(s_sc, (C - 1) * (16 * 2 * BC))
            add_agg(2 * C - 1, C - 1, rows3z)
            copy_zT(s_t2, s_zT, 2 * C - 1)
            gates_a(C - 1)
            gates_b(C - 1)

            def cast(ap, shape):
                return ap.to_broadcast(shape)

            nc.vector.tensor_tensor(out=pad_f[:, :], in0=seen[0:1, :], in1=region_e[0:1, :], op=ALU.add)
            link(nc.vector.tensor_tensor(out=has_t[:, :, :], in0=cast(seen[0:1, :].unsqueeze(2), [1, E, N // TS]),
                                         in1=cast(count_t[:, :].unsqueeze(1), [1, E, N // TS]), op=ALU.is_gt))
            nc.vector.tensor_copy(pad_at[:, :], pad_f[:, :]).then_inc(s_tab, 1)
            link(nc.vector.tensor_reduce(tiles_e[:, :], has_t[:, :, :], AX.X, ALU.add))
            nc.vector.tensor_scalar(skip_e[:, :], tiles_e[:, :], -float(TS), float(REGION), ALU.mult, ALU.add)
            link(nc.vector.tensor_tensor_scan(ends_e[:, :], one_e[:, :], tiles_e[:, :], 0.0, ALU.mult, ALU.add))
            link(nc.vector.tensor_tensor(out=past[:, :, :], in0=cast(ends_e[:, :].unsqueeze(1), [1, MT, E]),
                                         in1=cast(iota_m[:, :].unsqueeze(2), [1, MT, E]), op=ALU.is_le))
            nc.vector.tensor_reduce(tab_f[:, 1, :], past[:, :, :], AX.X, ALU.add)
            link(nc.vector.tensor_tensor(out=skipped[:, :, :], in0=past[:, :, :],
                                         in1=cast(skip_e[:, :].unsqueeze(1), [1, MT, E]), op=ALU.mult))
            link(nc.vector.tensor_reduce(tab_f[:, 0, :], skipped[:, :, :], AX.X, ALU.add))
            nc.vector.tensor_tensor(out=tab_f[:, 0, :], in0=tab_f[:, 0, :], in1=row_m[:, :], op=ALU.add)
            link(nc.vector.tensor_scalar(tab_f[:, 1, :], tab_f[:, 1, :], float(E - 1), None, ALU.min))
            nc.vector.tensor_copy(table[:, :, :], tab_f[:, :, :]).then_inc(s_tab, 1)

            def relu(m, slot, par):
                dve.wait_ge(s_up, 2 * m + 2)
                for k in range(K // 2, K):
                    last = nc.vector.tensor_scalar(hid[:, par, k, :], pHid[par][1][:, (k - K // 2) * TS:(k - K // 2 + 1) * TS],
                                                   wts[:, slot, K * (P + D) + k:K * (P + D) + k + 1], 0.0,
                                                   ALU.add, ALU.max)
                last.then_inc(s_hd, 1)

            def copy_in(m, par):
                dve.wait_ge(s_tr, m + 1)
                nc.vector.tensor_copy(zsT[:, par, :], pZ[par][:, 0:TS]).then_inc(s_zc, 1)

            def add_bias(m, slot, par):
                dve.wait_ge(s_dn, m + 1)
                nc.vector.tensor_tensor(out=yb2[:, slot, :, :], in0=pY[par][:, 0:S * D].rearrange("p (s d) -> p s d", s=S),
                                        in1=b2_t[:, slot, :].unsqueeze(1).to_broadcast([P, S, D]),
                                        op=ALU.add).then_inc(s_yb, 1)

            def step(m, u):
                if not isinstance(m, int) or m + 1 < MT:
                    relu(m + 1, (u + 1) % SLOTS, (u + 1) % 2)
                if not isinstance(m, int) or m + 2 < MT:
                    copy_in(m + 2, u % 2)
                add_bias(m, u % SLOTS, u % 2)

            copy_in(0, 0)
            relu(0, 0, 0)
            copy_in(1, 1)
            for m in range(SLOTS):
                step(m, m)
            with dve.Fori(1, MAIN) as i:
                for u in range(SLOTS):
                    step(i * SLOTS + u, u)
            for m in range(MAIN * SLOTS, MT):
                step(m, m)

            for c in range(C):
                dve.wait_ge(s_pk[c], 32)
                xc = xs[:, c * BC:(c + 1) * BC, :]
                for k in range(2):
                    o = (c * 2 + k) * BC * D
                    last = nc.vector.tensor_tensor(out=xc, in0=xc,
                                                   in1=pick_in[:, o:o + BC * D].rearrange("p (b d) -> p b d", b=BC),
                                                   op=ALU.add)
                    if k == 0:
                        link(last)
                last.then_inc(s_fin, 1)

        @block.tensor
        def _(pe):
            def group(n, g, feats, ready):
                ready()
                half = g * 2 // G
                if g * 2 % G == 0:
                    free = (s_half, s_agg)[half]
                    if isinstance(n, int):
                        if n:
                            pe.wait_ge(free, n)
                    else:
                        pe.wait_ge(free, n)
                for jj in range(J):
                    j = g * J + jj
                    last = nc.tensor.matmul(acc[half][:, :], feats[:, j, :], ring[:, g, jj * T:(jj + 1) * T],
                                            start=(j % (NB // 2) == 0), stop=(j % (NB // 2) == NB // 2 - 1))
                last.then_inc(s_grp, 1)

            def transposes(src, done):
                for b in range(BC):
                    last = nc.tensor.transpose(pT[:, b * P:(b + 1) * P], src(b), ident[:, :])
                last.then_inc(done, 1)

            def products(w, width, done):
                for b in range(BC):
                    last = nc.tensor.matmul(pF[:, b * width:(b + 1) * width], zT[:, b * P:(b + 1) * P], w,
                                            start=True, stop=True)
                last.then_inc(done, 1)

            def t1(n):
                pe.wait_ge(s_agg, n + 1)
                transposes(lambda b: aggT[:, b * P:(b + 1) * P], s_t1)

            def t2(n):
                pe.wait_ge(s_z1, n + 1)
                transposes(lambda b: z[:, b, :], s_t2)

            def ffn(n):
                pe.wait_ge(s_zT, n + 1)
                products(ffn_s[:, :], D, s_f)

            def t3(n):
                pe.wait_ge(s_z2, n + 1)
                transposes(lambda b: z[:, b, :], s_t3)

            def messages(n):
                pe.wait_ge(s_zT2, n + 1)
                products(gnn_s[:, :], D, s_m)

            def ranks(n):
                c = n - C
                pe.wait_ge(s_sel, c + 1)
                nc.tensor.matmul(pR[:, 0:(BC + 1) * E], before[:, :], both[:, :, :], start=True, stop=False)
                for b in range(BC):
                    last = nc.tensor.matmul(pR[:, (b + 1) * E:(BC + 1) * E], ones[:, :],
                                            both[:, b:b + 1, :].to_broadcast([P, BC - b, E]),
                                            start=False, stop=(b == BC - 1))
                last.then_inc(s_rk, 1)

            def t2r(n):
                pe.wait_ge(s_z1, n + 1)
                transposes(lambda b: rows3[:, 0, b, 0:D], s_t2)

            def gates(n):
                pe.wait_ge(s_zT, n + 1)
                products(gate_s[:, :], E, s_gt)

            pe.wait_ge(s_id, 2)
            for g in range(G):
                def ready():
                    pe.wait_ge(s_in[g], 16)
                    pe.wait_ge(s_h0, g + 1)
                group(0, g, h0, ready)
            pe.wait_ge(s_par, 96)

            STEPS0 = {0: t1, 2: t2, 3: ffn, 5: t3, 6: messages}
            STEPS1 = {1: t1, 3: t2r, 4: gates, 6: ranks}
            pe.wait_ge(s_cst, CST)
            with pe.Fori(1, C) as c:
                for g in range(G):
                    group(c, g, h0, lambda: pe.wait_ge(s_in[g], (c + 1) * 16))
                    if g in STEPS0:
                        STEPS0[g](c - 1)
            for g in range(G):
                def ready():
                    pe.wait_ge(s_wr, g + 1)
                    pe.wait_ge(s_msg, g + 1)
                group(C, g, msg, ready)
                if g in STEPS0:
                    STEPS0[g](C - 1)
            with pe.Fori(1, C) as c:
                for g in range(G):
                    group(c + C, g, msg, lambda: pe.wait_ge(s_wr, c * G + (g + 1)))
                    if g in STEPS1:
                        STEPS1[g](c + (C - 1))
            for g in STEPS1:
                STEPS1[g](2 * C - 1)

            def transpose_in(m, slot, par, turn):
                pe.wait_ge(s_srt[slot], (turn + 1) * 16)
                for s in range(S):
                    last = nc.tensor.transpose(pZ[par][:, s * P:(s + 1) * P], srt[:, slot, s, 0:D], ident[:, :])
                last.then_inc(s_tr, 1)

            def up(m, slot, par, turn):
                pe.wait_ge(s_wt[slot], (turn + 1) * 32)
                pe.wait_ge(s_zc, m + 1)
                for k in range(K):
                    last = nc.tensor.matmul(pHid[par][k * 2 // K][:, k % 2 * TS:(k % 2 + 1) * TS],
                                            wts[:, slot, k * P:(k + 1) * P], zsT[:, par, :], start=True, stop=True)
                    if k % 2:
                        last.then_inc(s_up, 1)

            def down(m, slot, par):
                pe.wait_ge(s_ha, m + 1)
                pe.wait_ge(s_hd, m + 1)
                if not isinstance(m, int) or m >= 2:
                    pe.wait_ge(s_yb, m - 1)
                for s in range(S):
                    for k in range(K):
                        last = nc.tensor.matmul(pY[par][:, s * D:(s + 1) * D], hid[:, par, k, s * P:(s + 1) * P],
                                                wts[:, slot, K * P + k * D:K * P + (k + 1) * D],
                                                start=(k == 0), stop=(k == K - 1))
                last.then_inc(s_dn, 1)

            def step(m, u, turn):
                if not isinstance(m, int) or m + 1 < MT:
                    up(m + 1, (u + 1) % SLOTS, (u + 1) % 2, turn + (u + 1) // SLOTS)
                if not isinstance(m, int) or m + 2 < MT:
                    transpose_in(m + 2, (u + 2) % SLOTS, u % 2, turn + (u + 2) // SLOTS)
                down(m, u, u % 2)

            transpose_in(0, 0, 0, 0)
            up(0, 0, 0, 0)
            transpose_in(1, 1, 1, 0)
            for u in range(SLOTS):
                step(u, u, 0)
            with pe.Fori(1, MAIN) as i:
                for u in range(SLOTS):
                    step(i * SLOTS + u, u, i)
            for m in range(MAIN * SLOTS, MT):
                step(m, m % SLOTS, m // SLOTS)


def kernel(**inputs):
    import numpy as _np
    import concourse.bacc as _bacc
    from concourse import mybir as _mybir
    from concourse.bass_utils import run_bass_kernel_spmd as _run

    P, T, J = 128, 512, 4
    a = {k: _np.asarray(v) for k, v in inputs.items()}
    n, d = a["x"].shape
    e, h = a["L1_ffn_b1"].shape
    laid = {
        "x": a["x"],
        "adjT": a["adj"].reshape(n // T, T, n // (J * P), J, P).transpose(0, 2, 4, 3, 1).reshape(n // T, n // (J * P), P, J * T),
        "w_l0": a["L0_gnn_W"],
        "ffn_wT": a["L0_ffn_weight"].T,
        "ffn_b": a["L0_ffn_bias"],
        "gnn_w": a["L1_gnn_W"],
        "gnn_b": a["L1_gnn_B"],
        "gate_wT": a["L1_ffn_Wg"].T,
        "gate_b": a["L1_ffn_bg"],
        "experts": _np.concatenate([
            a["L1_ffn_W1"].transpose(0, 2, 1),
            a["L1_ffn_W2"].reshape(e, d, h // P, P).transpose(0, 3, 2, 1).reshape(e, P, h // P * d),
            a["L1_ffn_b1"].reshape(e, h // P, P).transpose(0, 2, 1)], axis=2),
        "b2": a["L1_ffn_b2"],
    }
    nc = _bacc.Bacc("TRN2", target_bir_lowering=False, num_devices=1)
    arrays, args = {}, []
    for name, v in laid.items():
        v = _np.ascontiguousarray(v)
        arrays[f"in_{name}"] = v
        args.append(nc.dram_tensor(f"in_{name}", v.shape, _mybir.dt.from_np(v.dtype), kind="ExternalInput").ap())
    out = nc.dram_tensor("out_0", (n, d), _mybir.dt.from_np(a["x"].dtype), kind="ExternalOutput").ap()
    gnn_ffn_gnn_moe_kernel(nc, *args, out)
    r = _run(nc, [arrays], core_ids=[0])
    return r.results[0]["out_0"]
```

```python
import concourse.bass as bass
from concourse import mybir
from contextlib import ExitStack


def gnn_ffn_gnn_moe_kernel(
    nc: bass.Bass,
    x: bass.AP,
    adjT: bass.AP,
    w_l0: bass.AP,
    ffn_wT: bass.AP,
    ffn_b: bass.AP,
    gnn_w: bass.AP,
    gnn_b: bass.AP,
    gate_wT: bass.AP,
    gate_b: bass.AP,
    experts: bass.AP,
    b2: bass.AP,
    out: bass.AP,
):
    f32 = mybir.dt.float32
    i32 = mybir.dt.int32
    u32 = mybir.dt.uint32
    ALU = mybir.AluOpType
    ACT = mybir.ActivationFunctionType
    AX = mybir.AxisListType

    P = 128
    D = x.shape[1]
    N = x.shape[0]
    NB = N // P
    C, G = adjT.shape[0], adjT.shape[1]
    T = N // C
    BC = T // P
    J = NB // G
    GT = J * T
    E = gate_b.shape[0]
    K = experts.shape[2] // (P + D + 1)
    S = 2
    TS = S * P
    MT = 2 * N // TS + E - 1
    REGION = N + TS
    DUMMY = MT - 2 * N // TS
    RW = D + 2
    SLOTS = 8
    EPS = 1e-5
    TINY = 2.0 ** -60
    MAGIC = float(0x5F3759DF)
    EARLY = 3
    LATE = G - EARLY
    BY_POOL = 6
    SQUARES = 3

    ctx = ExitStack()
    with ctx:
        def sb(name, shape, dt=f32):
            return ctx.enter_context(nc.sbuf_tensor(name, shape, dt))

        def pb(name):
            return ctx.enter_context(nc.psum_tensor(name, [P, 512], f32))

        def sem(name):
            return ctx.enter_context(nc.semaphore(name))

        xs = sb("xs", [P, NB, D])
        h0 = sb("h0", [P, NB, D])
        msg = sb("msg", [P, NB, D])
        ring = sb("ring", [P, G, GT])
        kept = sb("kept", [P, C, GT])
        ffn_s = sb("ffn_s", [P, D])
        gnn_s = sb("gnn_s", [P, D])
        gate_s = sb("gate_s", [P, E])
        w_row = sb("w_row", [P, D])
        ffnb_row = sb("ffnb_row", [P, D])
        gnnb_row = sb("gnnb_row", [P, D])
        gateb_row = sb("gateb_row", [P, E])
        ident = sb("ident", [P, P])
        before = sb("before", [P, P])
        ones = sb("ones", [P, P])
        iota_e = sb("iota_e", [P, E])
        region_e = sb("region_e", [P, E])
        out_row = sb("out_row", [P, 2, BC], i32)
        first_row = sb("first_row", [P, 2, BC], i32)
        step_row = sb("step_row", [P, 2, BC], i32)
        count_t = sb("count_t", [1, N // TS])
        iota_m = sb("iota_m", [1, MT])
        row_m = sb("row_m", [1, MT])
        nothing = sb("nothing", [P, 1], i32)
        carrier = sb("carrier", [P, SLOTS, 1], i32)
        padding = sb("padding", [P, S, RW])
        aggT = sb("aggT", [P, T])
        z = sb("z", [P, BC, D])
        zT = sb("zT", [P, T])
        stats = sb("stats", [P, NB - BC, 6])
        mv = sb("mv", [P, NB - BC, 2])
        va, hv, ta, ua, ea, yb = (sb(name, [P, NB - BC]) for name in ("va", "hv", "ta", "ua", "ea", "yb"))
        sc = sb("sc", [P, BC, E])
        top = sb("top", [P, BC, 8])
        topi = sb("topi", [P, BC, 8], u32)
        topf = sb("topf", [P, BC, 2])
        gap = sb("gap", [P, BC])
        eg = sb("eg", [P, BC])
        den = sb("den", [P, BC])
        rows3 = sb("rows3", [P, 2, BC, RW])
        sel = sb("sel", [P, 2, BC, E])
        both = sb("both", [P, BC + 1, E])
        rank = sb("rank", [P, BC + 1, E])
        seen = sb("seen", [P, E])
        prow = sb("prow", [P, BC, E])
        posf = sb("posf", [P, 2, BC])
        posu = sb("posu", [P, 2, BC], u32)
        has_t = sb("has_t", [1, E, N // TS])
        tiles_e = sb("tiles_e", [1, E])
        ends_e = sb("ends_e", [1, E])
        one_e = sb("one_e", [1, E])
        skip_e = sb("skip_e", [1, E])
        past = sb("past", [1, MT, E])
        skipped = sb("skipped", [1, MT, E])
        tab_f = sb("tab_f", [1, 2, MT])
        table = sb("table", [1, 2, MT], i32)
        pad_f = sb("pad_f", [1, E])
        pad_at = sb("pad_at", [1, E], i32)
        free = kept[:, :, :].rearrange("p c n -> p (c n)")
        used = 0

        def part(*shape):
            nonlocal used
            size = 1
            for length in shape:
                size *= length
            used += size
            assert used <= C * GT
            names = " ".join("abc"[:len(shape)])
            return free[:, used - size:used].rearrange(f"p ({names}) -> p {names}",
                                                       **dict(zip("abc", shape)))

        srt = part(SLOTS, S, RW)
        wts = part(SLOTS, K * (P + D + 1))
        b2_t = part(SLOTS, D)
        zsT = part(2, TS)
        hid = part(2, K, TS)
        yb2 = part(2, S, D)
        ysc = h0[:, 0:SLOTS * S, :].rearrange("p (a b) c -> p a b c", a=SLOTS)
        pick_in = ring[:, :, :].rearrange("p g n -> p (g n)")

        sorted_rows = nc.dram_tensor("sorted_rows", [E * REGION + DUMMY * TS, RW], f32).ap()
        early = nc.dram_tensor("early", [C, EARLY - 1, P, GT], f32).ap()
        picked = nc.dram_tensor("picked", [2 * N, D], f32).ap()

        acc = [pb("accA"), pb("accB")]
        pT = pb("pT")
        pF = pb("pF")
        pR = pb("pR")
        pH = pb("pH")
        pY = [pb("pY0"), pb("pY1")]
        pHid = [acc, [pR, pH]]
        pZ = [pT, pF]

        s_x = sem("s_x")
        s_xr = sem("s_xr")
        s_par = sem("s_par")
        s_in = [sem(f"s_in{g}") for g in range(G)]
        s_id = sem("s_id")
        s_h0 = sem("s_h0")
        s_grp = sem("s_grp")
        s_half = sem("s_half")
        s_agg = sem("s_agg")
        s_t1 = sem("s_t1")
        s_z1 = sem("s_z1")
        s_t2 = sem("s_t2")
        s_zT = sem("s_zT")
        s_f = sem("s_f")
        s_z2 = sem("s_z2")
        s_t3 = sem("s_t3")
        s_zT2 = sem("s_zT2")
        s_m = sem("s_m")
        s_msg = sem("s_msg")
        s_mask = sem("s_mask")
        s_less = sem("s_less")
        s_pmask = sem("s_pmask")
        s_keep = sem("s_keep")
        s_new = sem("s_new")
        s_st = [sem(f"s_st{g}") for g in range(EARLY)]
        s_act = sem("s_act")
        s_inv = sem("s_inv")
        s_sq = sem("s_sq")
        s_wr = sem("s_wr")
        s_gt = sem("s_gt")
        s_gap = sem("s_gap")
        s_eg = sem("s_eg")
        s_cst = sem("s_cst")
        s_pad0 = sem("s_pad0")
        s_sel = sem("s_sel")
        s_rk = sem("s_rk")
        s_pos = sem("s_pos")
        s_sc = sem("s_sc")
        s_tab = sem("s_tab")
        s_pad = sem("s_pad")
        s_srt = [sem(f"s_srt{i}") for i in range(SLOTS)]
        s_wt = [sem(f"s_wt{i}") for i in range(SLOTS)]
        s_tr = sem("s_tr")
        s_zc = sem("s_zc")
        s_up = sem("s_up")
        s_ha = sem("s_ha")
        s_hd = sem("s_hd")
        s_dn = sem("s_dn")
        s_yb = sem("s_yb")
        s_pr = sem("s_pr")
        s_took = sem("s_took")
        s_ysc = [sem(f"s_ysc{i}") for i in range(SLOTS)]
        s_pk = [sem(f"s_pk{c}") for c in range(C)]
        s_fin = sem("s_fin")
        s_out = sem("s_out")

        CST = 16
        MAIN = (MT - 2) // SLOTS

        block = ctx.enter_context(nc.Block())

        def at(m):
            return slice(m, m + 1) if isinstance(m, int) else bass.ds(m, 1)

        def pad(eng, e):
            row = eng.value_load(pad_at[0:1, e:e + 1], min_val=0, max_val=E * REGION - TS)
            eng.dma_start(sorted_rows[bass.ds(row, TS), :].rearrange("(p s) d -> p s d", s=S),
                          padding[:, :, :]).then_inc(s_pad, 16)

        @block.sync
        def _(sp):
            xv = x.rearrange("(b p) d -> p b d", p=P)
            sp.dma_start(xs[:, 0:BC, :], xv[:, 0:BC, :]).then_inc(s_x, 16)
            sp.dma_start(w_row[:, :], w_l0.partition_broadcast(P)).then_inc(s_x, 16)
            sp.dma_start(xs[:, BC:NB, :], xv[:, BC:NB, :]).then_inc(s_xr, 16)
            for g in range(G):
                sp.dma_start(ring[:, g, :], adjT[0, g]).then_inc(s_in[g], 16)
            with sp.Fori(0, C - 1) as c:
                def store(g):
                    sp.wait_ge(s_new, c * (EARLY - 1) + g)
                    sp.dma_start(early[c, g - 1], ring[:, g, :]).then_inc(s_st[g], 16)

                def load(g):
                    if g == 0:
                        sp.wait_ge(s_keep, c + 1)
                    elif g < EARLY:
                        sp.wait_ge(s_st[g], (c + 1) * 16)
                    else:
                        sp.wait_ge(s_grp, c * G + (g + 1))
                    sp.dma_start(ring[:, g, :], adjT[c + 1, g]).then_inc(s_in[g], 16)

                load(0)
                load(3)
                store(1)
                load(4)
                load(1)
                store(2)
                load(5)
                load(2)
                load(6)
                load(7)

            def store_last(g):
                sp.wait_ge(s_new, (C - 1) * (EARLY - 1) + g)
                sp.dma_start(early[C - 1, g - 1], ring[:, g, :]).then_inc(s_st[g], 16)

            def load_first(g):
                if g < EARLY:
                    sp.wait_ge(s_st[g], C * 16)
                else:
                    sp.wait_ge(s_grp, (C - 1) * G + (g + 1))
                sp.dma_start(ring[:, g, :], early[0, g - 1] if g < EARLY else adjT[0, g]).then_inc(s_in[g], 16)

            load_first(3)
            store_last(1)
            load_first(4)
            load_first(5)
            store_last(2)
            load_first(6)
            load_first(1)
            load_first(2)
            load_first(7)
            with sp.Fori(1, C) as c:
                for g in range(1, G):
                    sp.wait_ge(s_grp, (c + (C - 1)) * G + (g + 1))
                    sp.dma_start(ring[:, g, :], early[c, g - 1] if g < EARLY else adjT[c, g]).then_inc(s_in[g], 16)

            sp.wait_ge(s_tab, 1)
            for e in range(0, E, 2):
                pad(sp, e)

            def load_tile(m, slot, turn):
                first = sp.value_load(table[0:1, 0:1, at(m)], min_val=0, max_val=E * REGION + (DUMMY - 1) * TS)
                expert = sp.value_load(table[0:1, 1:2, at(m)], min_val=0, max_val=E - 1)
                if turn is not None:
                    sp.wait_ge(s_dn, m - (SLOTS - 1))
                    sp.wait_ge(s_yb, m - (SLOTS - 1))
                sp.dma_start(wts[:, slot, :], experts[bass.ds(expert, 1), :, :].rearrange("a p n -> (a p) n")
                             ).then_inc(s_wt[slot], 16)
                sp.dma_start(b2_t[:, slot, :], b2[bass.ds(expert, 1), :].rearrange("a d -> (a d)")
                             .partition_broadcast(P)).then_inc(s_wt[slot], 16)
                if turn is not None:
                    sp.wait_ge(s_ysc[slot], turn * (16 * S))
                elif slot == 0:
                    sp.wait_ge(s_pad, 16 * E)
                    sp.wait_ge(s_sc, 16 * 2 * NB)
                    sp.wait_ge(s_pad0, 16 * DUMMY)
                sp.dma_start(srt[:, slot, :, :], sorted_rows[bass.ds(first, TS), :].rearrange("(p s) d -> p s d", s=S)
                             ).then_inc(s_srt[slot], 16)

            sp.wait_ge(s_tab, 2)
            for m in range(SLOTS):
                load_tile(m, m, None)
            with sp.Fori(1, MT // SLOTS) as i:
                for u in range(SLOTS):
                    load_tile(i * SLOTS + u, u, i)
            for m in range(MT // SLOTS * SLOTS, MT):
                load_tile(m, m % SLOTS, m // SLOTS)

            for i in range(SLOTS):
                sp.wait_ge(s_ysc[i], 16 * S * ((MT - i + SLOTS - 1) // SLOTS))
            for c in range(C):
                for k in range(2):
                    sp.dma_start(pick_in[:, (c * 2 + k) * BC * D:(c * 2 + k + 1) * BC * D]
                                 .rearrange("p (b d) -> p b d", b=BC),
                                 picked[k * N + c * T:k * N + (c + 1) * T, :].rearrange("(b p) d -> p b d", p=P)
                                 ).then_inc(s_pk[c], 16)
            for c in range(C):
                sp.wait_ge(s_fin, c + 1)
                sp.dma_start(out[c * T:(c + 1) * T, :].rearrange("(b p) d -> p b d", p=P),
                             xs[:, c * BC:(c + 1) * BC, :]).then_inc(s_out, 16)
            sp.wait_ge(s_out, 16 * C)

        @block.gpsimd
        def _(pool):
            nc.gpsimd.memset(ident[:, :], 0.0).then_inc(s_id, 1)
            pool.wait_ge(s_id, 1)
            nc.gpsimd.affine_select(out=ident[:, :], in_=ident[:, :], compare_op=ALU.not_equal, fill=1.0,
                                    base=0, pattern=[[-1, P]], channel_multiplier=1).then_inc(s_id, 1)
            nc.gpsimd.memset(ones[:, :], 1.0).then_inc(s_cst, 1)
            pool.wait_ge(s_cst, 1)
            nc.gpsimd.affine_select(out=before[:, :], in_=ones[:, :], compare_op=ALU.is_gt, fill=0.0,
                                    base=0, pattern=[[1, P]], channel_multiplier=-1).then_inc(s_cst, 1)
            for dst, pattern, channel in ((iota_e[:, :], [[1, E]], 0), (region_e[:, :], [[REGION, E]], 0),
                                          (out_row[:, :, :], [[N, 2], [P, BC]], 1),
                                          (count_t[:, :], [[TS, N // TS]], 0), (iota_m[:, :], [[1, MT]], 0),
                                          (row_m[:, :], [[TS, MT]], 0)):
                nc.gpsimd.iota(dst, pattern=pattern, base=0, channel_multiplier=channel,
                               allow_small_or_imprecise_dtypes=True).then_inc(s_cst, 1)
            for dst, value in ((both[:, :, :], 0.0), (seen[:, :], 0.0), (one_e[:, :], 1.0),
                               (padding[:, :, 0:D + 1], 0.0)):
                nc.gpsimd.memset(dst, value).then_inc(s_cst, 1)
            nc.gpsimd.memset(padding[:, :, D + 1:RW].bitcast(i32), 2 * N).then_inc(s_cst, 1)
            nc.gpsimd.memset(first_row[:, :, :], 0).then_inc(s_cst, 1)
            nc.gpsimd.memset(nothing[:, :], 0).then_inc(s_cst, 1)
            nc.gpsimd.memset(step_row[:, :, :], T).then_inc(s_cst, 1)
            pool.wait_ge(s_cst, CST)

            less = h0[:, 0:GT // D, :].rearrange("p b d -> p (b d)")

            def mask(c):
                pool.wait_ge(s_in[BY_POOL], 16 * (c + (C + 1)))
                nc.gpsimd.tensor_tensor(out=carrier[:, 0, :], in0=nothing[:, :], in1=nothing[:, :], op=ALU.add)
                nc.gpsimd.tensor_scalar(less, ring[:, BY_POOL, :], 1.0, None, ALU.is_lt).then_inc(s_less, 1)
                pool.wait_ge(s_less, c + 1)
                nc.gpsimd.tensor_tensor(out=ring[:, BY_POOL, :], in0=ring[:, BY_POOL, :], in1=less,
                                        op=ALU.mult).then_inc(s_pmask, 1)

            def scatter_rows(c):
                pool.wait_ge(s_pos, c + 1)
                nc.gpsimd.tensor_tensor(out=rows3[:, :, :, D + 1].bitcast(i32), in0=out_row[:, :, :],
                                        in1=first_row[:, :, :], op=ALU.add)
                pool.drain()
                nc.gpsimd.tensor_tensor(out=first_row[:, :, :], in0=first_row[:, :, :], in1=step_row[:, :, :],
                                        op=ALU.add)
                pool.drain()
                for k in range(2):
                    for b in range(BC):
                        nc.gpsimd.indirect_dma_start(
                            out=sorted_rows, out_offset=bass.IndirectOffsetOnAxis(ap=posu[:, k, b:b + 1], axis=0),
                            in_=rows3[:, k, b, :], in_offset=None).then_inc(s_sc, 16)

            mask(0)
            with pool.Fori(1, C) as c:
                mask(c)
                scatter_rows(c - 1)
            scatter_rows(C - 1)

            def store_tile(m, slot):
                pool.wait_ge(s_pr, m + 1)
                nc.gpsimd.tensor_tensor(out=carrier[:, slot, :], in0=nothing[:, :], in1=nothing[:, :],
                                        op=ALU.add).then_inc(s_took, 1)
                for s in range(S):
                    nc.gpsimd.indirect_dma_start(
                        out=picked,
                        out_offset=bass.IndirectOffsetOnAxis(ap=srt[:, slot, s, D + 1:RW].bitcast(u32), axis=0),
                        in_=ysc[:, slot, s, :], in_offset=None, bounds_check=2 * N - 1,
                        oob_is_err=False).then_inc(s_ysc[slot], 16)

            with pool.Fori(0, MT // SLOTS) as i:
                for u in range(SLOTS):
                    store_tile(i * SLOTS + u, u)
            for m in range(MT // SLOTS * SLOTS, MT):
                store_tile(m, m % SLOTS)

        @block.scalar
        def _(act):
            for dst, src in ((ffn_s, ffn_wT), (gnn_s, gnn_w), (gate_s, gate_wT)):
                act.dma_start(dst[:, :], src).then_inc(s_par, 16)
            for dst, src in ((ffnb_row, ffn_b), (gnnb_row, gnn_b), (gateb_row, gate_b)):
                act.dma_start(dst[:, :], src.partition_broadcast(P)).then_inc(s_par, 16)
            act.wait_ge(s_cst, CST)
            for i in range(DUMMY):
                row = E * REGION + i * TS
                act.dma_start(sorted_rows[row:row + TS, :].rearrange("(p s) d -> p s d", s=S),
                              padding[:, :, :]).then_inc(s_pad0, 16)
            act.preload_act_table_set("natural_log_exp_and_others")

            def copy_half(n):
                act.wait_ge(s_grp, n * G + G // 2)
                if not isinstance(n, int) or n:
                    act.wait_ge(s_t1, n)
                nc.scalar.copy(aggT[:, :], acc[0][:, :]).then_inc(s_half, 1)

            class chain:
                before, length, done = 0, 3 * EARLY - 1, 0

            def chained(c, ins):
                ins.then_inc(s_act, 1)
                chain.done += 1
                act.wait_ge(s_act, c * chain.length + (chain.before + chain.done))

            def invert(c, slot):
                chained(c, nc.scalar.activation(slot, slot, ACT.Ln, bias=TINY))
                chained(c, nc.scalar.activation(slot, slot, ACT.Exp, scale=-1.0))
                return nc.scalar.activation(slot, slot, ACT.Square, bias=-1.0)

            def early_weights(c):
                chain.done = 0
                for g in range(EARLY):
                    slot = ring[:, g, :]
                    act.wait_ge(s_mask, c * EARLY + (g + 1))
                    square = invert(c, slot)
                    if g == 0:
                        act.drain()
                        kc = kept[:, bass.ds(c, 1), :].rearrange("p c n -> p (c n)")
                        nc.scalar.activation(kc, slot, ACT.Exp, scale=-2.0).then_inc(s_keep, 1)
                    else:
                        chained(c, square)
                        nc.scalar.activation(slot, slot, ACT.Exp, scale=-2.0).then_inc(s_new, 1)
                    if g == 1:
                        copy_half(c)
                assert chain.done == chain.length

            def gate_exp(c):
                act.wait_ge(s_gap, c + 1)
                nc.scalar.activation(eg[:, :], gap[:, :], ACT.Exp).then_inc(s_eg, 1)

            def start(c, g):
                slot = ring[:, g, :]
                if g == BY_POOL:
                    act.wait_ge(s_pmask, c + 1)
                else:
                    act.wait_ge(s_mask, c * (LATE - 1) + (C * EARLY + g - EARLY + 1 - (g > BY_POOL)))
                chained(c, nc.scalar.activation(slot, slot, ACT.Ln, bias=TINY))
                inverse = nc.scalar.activation(slot, slot, ACT.Exp, scale=-1.0)
                if g < EARLY + SQUARES:
                    inverse.then_inc(s_inv, 1)
                else:
                    chained(c, inverse)

            def finish(c, g):
                slot = ring[:, g, :]
                if g < EARLY + SQUARES:
                    act.wait_ge(s_sq, c * SQUARES + (g - EARLY + 1))
                    bias = -2.0
                else:
                    chained(c, nc.scalar.activation(slot, slot, ACT.Square, bias=-1.0))
                    bias = 0.0
                nc.scalar.activation(slot, slot, ACT.Exp, scale=-2.0, bias=bias).then_inc(s_wr, 1)

            def late_weights(c, gate):
                chain.done = 0
                start(c, 3)
                start(c, 4)
                finish(c, 3)
                start(c, 5)
                finish(c, 4)
                start(c, 6)
                finish(c, 5)
                copy_half(c + C)
                finish(c, 6)
                if gate:
                    gate_exp(c - 1)
                start(c, 7)
                finish(c, 7)
                assert chain.done == chain.length

            early_weights(0)
            with act.Fori(1, C) as c:
                early_weights(c)
            chain.before, chain.length = C * chain.length, SQUARES + 3 * (LATE - SQUARES)
            late_weights(0, False)
            with act.Fori(1, C) as c:
                late_weights(c, True)
            gate_exp(C - 1)

            act.wait_ge(s_tab, 1)
            for e in range(1, E, 2):
                pad(act, e)

            def relu(m, slot, par):
                act.wait_ge(s_up, 2 * m + 1)
                for k in range(K // 2):
                    last = nc.scalar.activation(hid[:, par, k, :], pHid[par][0][:, k * TS:(k + 1) * TS], ACT.Relu,
                                                bias=wts[:, slot, K * (P + D) + k:K * (P + D) + k + 1])
                last.then_inc(s_ha, 1)

            def scale(m, slot, par):
                if not isinstance(m, int) or m >= SLOTS:
                    act.wait_ge(s_took, m - (SLOTS - 1))
                act.wait_ge(s_yb, m + 1)
                for k in range(S):
                    last = nc.scalar.activation(ysc[:, slot, k, :], yb2[:, par, k, :], ACT.Copy,
                                                scale=srt[:, slot, k, D:D + 1])
                last.then_inc(s_pr, 1)

            relu(0, 0, 0)
            for m in range(SLOTS):
                relu(m + 1, (m + 1) % SLOTS, (m + 1) % 2)
                scale(m, m, m % 2)
            with act.Fori(1, MAIN) as i:
                for u in range(SLOTS):
                    relu(i * SLOTS + (u + 1), (u + 1) % SLOTS, (u + 1) % 2)
                    scale(i * SLOTS + u, u, u % 2)
            for m in range(MAIN * SLOTS, MT):
                if m + 1 < MT:
                    relu(m + 1, (m + 1) % SLOTS, (m + 1) % 2)
                scale(m, m % SLOTS, m % 2)

        @block.vector
        def _(dve):
            def link(ins):
                dve.drain()

            def moments(src, count):
                for b in range(count):
                    last = nc.vector.bn_stats(stats[:, b, :], src[:, b, :])
                link(last)
                for b in range(count):
                    last = nc.vector.bn_aggr(mv[:, b, :], stats[:, b, :])
                link(last)

            def inverse_deviation(count):
                v, h, t, y, u, e = (a[:, 0:count] for a in (va, hv, ta, yb, ua, ea))
                nc.vector.tensor_scalar(h, mv[:, 0:count, 1], EPS, -0.5, ALU.add, ALU.mult)
                link(nc.vector.tensor_scalar(v, mv[:, 0:count, 1], EPS, None, ALU.add))
                link(nc.vector.tensor_scalar(t.bitcast(i32), v.bitcast(i32), 1, None, ALU.logical_shift_right))
                link(nc.vector.tensor_scalar(y.bitcast(i32), t.bitcast(i32), -1.0, MAGIC, ALU.mult, ALU.add))
                link(nc.vector.tensor_tensor(out=t, in0=y, in1=y, op=ALU.mult))
                link(nc.vector.tensor_tensor(out=e, in0=t, in1=h, op=ALU.mult))
                for newton in range(3):
                    last = nc.vector.scalar_tensor_tensor(out=y, in0=e, scalar=1.5, in1=y,
                                                          op0=ALU.add, op1=ALU.mult)
                    if newton < 2:
                        link(nc.vector.scalar_tensor_tensor(out=u, in0=e, scalar=1.5, in1=e,
                                                            op0=ALU.add, op1=ALU.mult))
                        last = nc.vector.scalar_tensor_tensor(out=e, in0=e, scalar=1.5, in1=u,
                                                              op0=ALU.add, op1=ALU.mult)
                    link(last)

            def normalise(src, dst, mean, inv):
                for b in range(BC):
                    last = nc.vector.tensor_scalar(dst[:, b, :], src[:, b, :], mean(b), inv(b),
                                                   ALU.subtract, ALU.mult)
                return last

            def layer_norm(src, dst):
                moments(src, BC)
                inverse_deviation(BC)
                return normalise(src, dst, lambda b: mv[:, b, 0:1], lambda b: yb[:, b:b + 1])

            def rows(row):
                return row[:, :].unsqueeze(1).to_broadcast([P, BC, row.shape[1]])

            def mask(g):
                nc.vector.scalar_tensor_tensor(out=ring[:, g, :], in0=ring[:, g, :], scalar=1.0,
                                               in1=ring[:, g, :], op0=ALU.is_lt,
                                               op1=ALU.mult).then_inc(s_mask, 1)

            def early_mask(c, g):
                dve.wait_ge(s_grp, c * G + (g + 1))
                mask(g)

            dve.wait_ge(s_x, 32)
            pv = pF[:, :].rearrange("p (b d) -> p b d", b=BC)
            tv = pT[:, :].rearrange("p (b d) -> p b d", b=BC)

            def times_w(blocks):
                nc.vector.tensor_tensor(out=h0[:, blocks, :], in0=h0[:, blocks, :], in1=rows(w_row),
                                        op=ALU.mult).then_inc(s_h0, 1)

            link(layer_norm(xs[:, 0:BC, :], h0))
            times_w(slice(0, BC))
            dve.wait_ge(s_xr, 16)
            moments(xs[:, BC:NB, :], NB - BC)
            inverse_deviation(NB - BC)
            for c in range(1, C):
                b0 = (c - 1) * BC
                link(normalise(xs[:, c * BC:(c + 1) * BC, :], h0[:, c * BC:(c + 1) * BC, :],
                               lambda b: mv[:, b0 + b, 0:1], lambda b: yb[:, b0 + b:b0 + b + 1]))
                times_w(slice(c * BC, (c + 1) * BC))
                if c % 2 and c // 2 < EARLY:
                    early_mask(0, c // 2)
            dve.wait_ge(s_par, 96)

            def span(c):
                return slice(c * BC, (c + 1) * BC) if isinstance(c, int) else bass.ds(c * BC, BC)

            def finish_agg(n):
                dve.wait_ge(s_half, n + 1)
                dve.wait_ge(s_grp, (n + 1) * G)
                nc.vector.tensor_tensor(out=aggT[:, :], in0=acc[1][:, :], in1=aggT[:, :],
                                        op=ALU.add).then_inc(s_agg, 1)

            def add_agg(n, c):
                xc = xs[:, span(c), :]
                dve.wait_ge(s_t1, n + 1)
                link(nc.vector.tensor_tensor(out=xc, in0=tv, in1=xc, op=ALU.add))
                layer_norm(xc, z).then_inc(s_z1, 1)

            def copy_zT(s_from, s_to, n):
                dve.wait_ge(s_from, n + 1)
                nc.vector.tensor_copy(zT[:, :], pT[:, :]).then_inc(s_to, 1)

            def post0_a(c):
                finish_agg(c)
                add_agg(c, c)

            def post0_b(c, between=None):
                xc = xs[:, bass.ds(c * BC, BC), :]
                copy_zT(s_t2, s_zT, c)
                if between:
                    between()
                link(nc.vector.tensor_tensor(out=xc, in0=xc, in1=rows(ffnb_row), op=ALU.add))
                dve.wait_ge(s_f, c + 1)
                link(nc.vector.tensor_tensor(out=xc, in0=pv, in1=xc, op=ALU.add))
                layer_norm(xc, z).then_inc(s_z2, 1)

            def post0_c(c):
                copy_zT(s_t3, s_zT2, c)
                dve.wait_ge(s_m, c + 1)
                nc.vector.tensor_tensor(out=msg[:, bass.ds(c * BC, BC), :], in0=pv, in1=rows(gnnb_row),
                                        op=ALU.add).then_inc(s_msg, 1)

            def late_mask(c, g):
                dve.wait_ge(s_in[g], 16 * (c + (C + 1)))
                mask(g)

            def square(c, g):
                dve.wait_ge(s_inv, c * SQUARES + (g - EARLY + 1))
                nc.vector.scalar_tensor_tensor(out=ring[:, g, :], in0=ring[:, g, :], scalar=-2.0,
                                               in1=ring[:, g, :], op0=ALU.add,
                                               op1=ALU.mult).then_inc(s_sq, 1)

            with dve.Fori(1, C) as c:
                finish_agg(c - 1)
                early_mask(c, 0)
                add_agg(c - 1, c - 1)
                early_mask(c, 1)
                post0_b(c - 1, lambda: early_mask(c, 2))
                post0_c(c - 1)

            def gates_a(c):
                dve.wait_ge(s_gt, c + 1)
                gv = pF[:, 0:BC * E].rearrange("p (b e) -> p b e", b=BC)
                link(nc.vector.tensor_tensor(out=sc[:, :, :], in0=gv, in1=rows(gateb_row), op=ALU.add))
                for b in range(BC):
                    last = nc.vector.max(top[:, b, :], sc[:, b, :])
                link(last)
                for b in range(BC):
                    last = nc.vector.max_index(topi[:, b, :], top[:, b, :], sc[:, b, :])
                link(last)
                nc.vector.tensor_tensor(out=gap[:, :], in0=top[:, :, 1], in1=top[:, :, 0],
                                        op=ALU.subtract).then_inc(s_gap, 1)
                link(nc.vector.tensor_copy(topf[:, :, :], topi[:, :, 0:2]))
                for k in range(2):
                    last = nc.vector.tensor_tensor(out=sel[:, k, :, :], in0=rows(iota_e),
                                                   in1=topf[:, :, k:k + 1].to_broadcast([P, BC, E]),
                                                   op=ALU.is_equal)
                link(last)
                nc.vector.tensor_tensor(out=both[:, 0:BC, :], in0=sel[:, 0, :, :], in1=sel[:, 1, :, :],
                                        op=ALU.add).then_inc(s_sel, 1)

            def gates_b(c, first):
                if not first:
                    dve.wait_ge(s_sc, c * (16 * 2 * BC))
                for k in range(2):
                    nc.vector.tensor_copy(rows3[:, k, :, 0:D], z[:, :, :])
                dve.wait_ge(s_eg, c + 1)
                link(nc.vector.tensor_scalar(den[:, :], eg[:, :], 1.0, None, ALU.add))
                link(nc.vector.reciprocal(rows3[:, 0, :, D], den[:, :]))
                nc.vector.tensor_tensor(out=rows3[:, 1, :, D], in0=eg[:, :], in1=rows3[:, 0, :, D], op=ALU.mult)
                dve.wait_ge(s_rk, c + 1)
                link(nc.vector.tensor_tensor(out=rank[:, :, :],
                                             in0=pR[:, 0:(BC + 1) * E].rearrange("p (b e) -> p b e", e=E),
                                             in1=seen[:, :].unsqueeze(1).to_broadcast([P, BC + 1, E]), op=ALU.add))
                link(nc.vector.tensor_tensor(out=rank[:, 0:BC, :], in0=rank[:, 0:BC, :], in1=rows(region_e),
                                             op=ALU.add))
                nc.vector.tensor_copy(seen[:, :], rank[:, BC, :])
                for k in range(2):
                    link(nc.vector.tensor_tensor(out=prow[:, :, :], in0=rank[:, 0:BC, :], in1=sel[:, k, :, :],
                                                 op=ALU.mult))
                    link(nc.vector.tensor_reduce(posf[:, k, :], prow[:, :, :], AX.X, ALU.add))
                nc.vector.tensor_copy(posu[:, :, :], posf[:, :, :]).then_inc(s_pos, 1)

            late_mask(0, 3)
            late_mask(0, 4)
            post0_a(C - 1)
            square(0, 3)
            late_mask(0, 5)
            square(0, 4)
            post0_b(C - 1)
            square(0, 5)
            post0_c(C - 1)
            late_mask(0, 7)
            dve.wait_ge(s_cst, CST)

            def weights_pass(c):
                late_mask(c, 3)
                late_mask(c, 4)
                late_mask(c, 5)
                square(c, 3)
                finish_agg(c + (C - 1))
                square(c, 4)
                add_agg(c + (C - 1), c - 1)
                square(c, 5)
                copy_zT(s_t2, s_zT, c + (C - 1))
                late_mask(c, 7)
                gates_a(c - 1)
                gates_b(c - 1, isinstance(c, int))

            weights_pass(1)
            with dve.Fori(2, C) as c:
                weights_pass(c)
            finish_agg(2 * C - 1)
            add_agg(2 * C - 1, C - 1)
            copy_zT(s_t2, s_zT, 2 * C - 1)
            gates_a(C - 1)
            gates_b(C - 1, False)

            def cast(ap, shape):
                return ap.to_broadcast(shape)

            nc.vector.tensor_tensor(out=pad_f[:, :], in0=seen[0:1, :], in1=region_e[0:1, :], op=ALU.add)
            link(nc.vector.tensor_tensor(out=has_t[:, :, :], in0=cast(seen[0:1, :].unsqueeze(2), [1, E, N // TS]),
                                         in1=cast(count_t[:, :].unsqueeze(1), [1, E, N // TS]), op=ALU.is_gt))
            nc.vector.tensor_copy(pad_at[:, :], pad_f[:, :]).then_inc(s_tab, 1)
            link(nc.vector.tensor_reduce(tiles_e[:, :], has_t[:, :, :], AX.X, ALU.add))
            nc.vector.tensor_scalar(skip_e[:, :], tiles_e[:, :], -float(TS), float(REGION), ALU.mult, ALU.add)
            link(nc.vector.tensor_tensor_scan(ends_e[:, :], one_e[:, :], tiles_e[:, :], 0.0, ALU.mult, ALU.add))
            link(nc.vector.tensor_tensor(out=past[:, :, :], in0=cast(ends_e[:, :].unsqueeze(1), [1, MT, E]),
                                         in1=cast(iota_m[:, :].unsqueeze(2), [1, MT, E]), op=ALU.is_le))
            nc.vector.tensor_reduce(tab_f[:, 1, :], past[:, :, :], AX.X, ALU.add)
            link(nc.vector.tensor_tensor(out=skipped[:, :, :], in0=past[:, :, :],
                                         in1=cast(skip_e[:, :].unsqueeze(1), [1, MT, E]), op=ALU.mult))
            link(nc.vector.tensor_reduce(tab_f[:, 0, :], skipped[:, :, :], AX.X, ALU.add))
            nc.vector.tensor_tensor(out=tab_f[:, 0, :], in0=tab_f[:, 0, :], in1=row_m[:, :], op=ALU.add)
            link(nc.vector.tensor_scalar(tab_f[:, 1, :], tab_f[:, 1, :], float(E - 1), None, ALU.min))
            nc.vector.tensor_copy(table[:, :, :], tab_f[:, :, :]).then_inc(s_tab, 1)

            def relu(m, slot, par):
                dve.wait_ge(s_up, 2 * m + 2)
                for k in range(K // 2, K):
                    last = nc.vector.tensor_scalar(hid[:, par, k, :], pHid[par][1][:, (k - K // 2) * TS:(k - K // 2 + 1) * TS],
                                                   wts[:, slot, K * (P + D) + k:K * (P + D) + k + 1], 0.0,
                                                   ALU.add, ALU.max)
                last.then_inc(s_hd, 1)

            def copy_in(m, par):
                dve.wait_ge(s_tr, m + 1)
                nc.vector.tensor_copy(zsT[:, par, :], pZ[par][:, 0:TS]).then_inc(s_zc, 1)

            def add_bias(m, slot, par):
                dve.wait_ge(s_dn, m + 1)
                if not isinstance(m, int) or m >= 2:
                    dve.wait_ge(s_pr, m - 1)
                nc.vector.tensor_tensor(out=yb2[:, par, :, :], in0=pY[par][:, 0:S * D].rearrange("p (s d) -> p s d", s=S),
                                        in1=b2_t[:, slot, :].unsqueeze(1).to_broadcast([P, S, D]),
                                        op=ALU.add).then_inc(s_yb, 1)

            def step(m, u):
                if not isinstance(m, int) or m + 1 < MT:
                    relu(m + 1, (u + 1) % SLOTS, (u + 1) % 2)
                if not isinstance(m, int) or m + 2 < MT:
                    copy_in(m + 2, u % 2)
                add_bias(m, u % SLOTS, u % 2)

            copy_in(0, 0)
            relu(0, 0, 0)
            copy_in(1, 1)
            for m in range(SLOTS):
                step(m, m)
            with dve.Fori(1, MAIN) as i:
                for u in range(SLOTS):
                    step(i * SLOTS + u, u)
            for m in range(MAIN * SLOTS, MT):
                step(m, m)

            for c in range(C):
                dve.wait_ge(s_pk[c], 32)
                xc = xs[:, c * BC:(c + 1) * BC, :]
                for k in range(2):
                    o = (c * 2 + k) * BC * D
                    last = nc.vector.tensor_tensor(out=xc, in0=xc,
                                                   in1=pick_in[:, o:o + BC * D].rearrange("p (b d) -> p b d", b=BC),
                                                   op=ALU.add)
                    if k == 0:
                        link(last)
                last.then_inc(s_fin, 1)

        @block.tensor
        def _(pe):
            def group(n, g, feats, ready, tiles=None):
                tiles = ring[:, g, :] if tiles is None else tiles
                ready()
                half = g * 2 // G
                if g * 2 % G == 0:
                    free = (s_half, s_agg)[half]
                    if isinstance(n, int):
                        if n:
                            pe.wait_ge(free, n)
                    else:
                        pe.wait_ge(free, n)
                for jj in range(J):
                    j = g * J + jj
                    last = nc.tensor.matmul(acc[half][:, :], feats[:, j, :], tiles[:, jj * T:(jj + 1) * T],
                                            start=(j % (NB // 2) == 0), stop=(j % (NB // 2) == NB // 2 - 1))
                last.then_inc(s_grp, 1)

            def transposes(src, done):
                for b in range(BC):
                    last = nc.tensor.transpose(pT[:, b * P:(b + 1) * P], src(b), ident[:, :])
                last.then_inc(done, 1)

            def products(w, width, done):
                for b in range(BC):
                    last = nc.tensor.matmul(pF[:, b * width:(b + 1) * width], zT[:, b * P:(b + 1) * P], w,
                                            start=True, stop=True)
                last.then_inc(done, 1)

            def t1(n):
                pe.wait_ge(s_agg, n + 1)
                transposes(lambda b: aggT[:, b * P:(b + 1) * P], s_t1)

            def t2(n):
                pe.wait_ge(s_z1, n + 1)
                transposes(lambda b: z[:, b, :], s_t2)

            def ffn(n):
                pe.wait_ge(s_zT, n + 1)
                products(ffn_s[:, :], D, s_f)

            def t3(n):
                pe.wait_ge(s_z2, n + 1)
                transposes(lambda b: z[:, b, :], s_t3)

            def messages(n):
                pe.wait_ge(s_zT2, n + 1)
                products(gnn_s[:, :], D, s_m)

            def ranks(n):
                c = n - C
                pe.wait_ge(s_sel, c + 1)
                nc.tensor.matmul(pR[:, 0:(BC + 1) * E], before[:, :], both[:, :, :], start=True, stop=False)
                for b in range(BC):
                    last = nc.tensor.matmul(pR[:, (b + 1) * E:(BC + 1) * E], ones[:, :],
                                            both[:, b:b + 1, :].to_broadcast([P, BC - b, E]),
                                            start=False, stop=(b == BC - 1))
                last.then_inc(s_rk, 1)

            def gates(n):
                pe.wait_ge(s_zT, n + 1)
                products(gate_s[:, :], E, s_gt)

            pe.wait_ge(s_id, 2)
            for g in range(G):
                def ready():
                    pe.wait_ge(s_in[g], 16)
                    pe.wait_ge(s_h0, g + 1)
                group(0, g, h0, ready)
            pe.wait_ge(s_par, 96)

            STEPS0 = {0: t1, 2: t2, 3: ffn, 5: t3, 6: messages}
            STEPS01 = {0: t1, 1: t2, 2: ffn, 3: t3, 4: messages}
            STEPS1 = {0: t1, 2: t2, 4: gates, 5: ranks}
            pe.wait_ge(s_cst, CST)
            with pe.Fori(1, C) as c:
                for g in range(G):
                    group(c, g, h0, lambda: pe.wait_ge(s_in[g], (c + 1) * 16))
                    if g in STEPS0:
                        STEPS0[g](c - 1)

            def weighted(c, g):
                def ready():
                    if g == 0:
                        if isinstance(c, int):
                            pe.wait_ge(s_keep, C)
                    elif g < EARLY:
                        pe.wait_ge(s_in[g], (c + (C + 1)) * 16)
                    else:
                        pe.wait_ge(s_wr, c * LATE + (g - EARLY + 1))
                    if isinstance(c, int):
                        pe.wait_ge(s_msg, g + 1)
                tiles = kept[:, at(c), :].rearrange("p c n -> p (c n)") if g == 0 else None
                group(c + C, g, msg, ready, tiles)

            for g in range(G):
                weighted(0, g)
                if g in STEPS01:
                    STEPS01[g](C - 1)
            with pe.Fori(1, C) as c:
                for g in range(G):
                    weighted(c, g)
                    if g in STEPS1:
                        STEPS1[g](c + (C - 1))
            for g in STEPS1:
                STEPS1[g](2 * C - 1)

            def transpose_in(m, slot, par, turn):
                pe.wait_ge(s_srt[slot], (turn + 1) * 16)
                for s in range(S):
                    last = nc.tensor.transpose(pZ[par][:, s * P:(s + 1) * P], srt[:, slot, s, 0:D], ident[:, :])
                last.then_inc(s_tr, 1)

            def up(m, slot, par, turn):
                pe.wait_ge(s_wt[slot], (turn + 1) * 32)
                pe.wait_ge(s_zc, m + 1)
                for k in range(K):
                    last = nc.tensor.matmul(pHid[par][k * 2 // K][:, k % 2 * TS:(k % 2 + 1) * TS],
                                            wts[:, slot, k * P:(k + 1) * P], zsT[:, par, :], start=True, stop=True)
                    if k % 2:
                        last.then_inc(s_up, 1)

            def down(m, slot, par):
                pe.wait_ge(s_ha, m + 1)
                pe.wait_ge(s_hd, m + 1)
                if not isinstance(m, int) or m >= 2:
                    pe.wait_ge(s_yb, m - 1)
                for s in range(S):
                    for k in range(K):
                        last = nc.tensor.matmul(pY[par][:, s * D:(s + 1) * D], hid[:, par, k, s * P:(s + 1) * P],
                                                wts[:, slot, K * P + k * D:K * P + (k + 1) * D],
                                                start=(k == 0), stop=(k == K - 1))
                last.then_inc(s_dn, 1)

            def step(m, u, turn):
                if not isinstance(m, int) or m + 1 < MT:
                    up(m + 1, (u + 1) % SLOTS, (u + 1) % 2, turn + (u + 1) // SLOTS)
                if not isinstance(m, int) or m + 2 < MT:
                    transpose_in(m + 2, (u + 2) % SLOTS, u % 2, turn + (u + 2) // SLOTS)
                down(m, u, u % 2)

            transpose_in(0, 0, 0, 0)
            up(0, 0, 0, 0)
            transpose_in(1, 1, 1, 0)
            for u in range(SLOTS):
                step(u, u, 0)
            with pe.Fori(1, MAIN) as i:
                for u in range(SLOTS):
                    step(i * SLOTS + u, u, i)
            for m in range(MAIN * SLOTS, MT):
                step(m, m % SLOTS, m // SLOTS)


def kernel(**inputs):
    import numpy as _np
    import concourse.bacc as _bacc
    from concourse import mybir as _mybir
    from concourse.bass_utils import run_bass_kernel_spmd as _run

    P, T, J = 128, 512, 4
    a = {k: _np.asarray(v) for k, v in inputs.items()}
    n, d = a["x"].shape
    e, h = a["L1_ffn_b1"].shape
    laid = {
        "x": a["x"],
        "adjT": a["adj"].reshape(n // T, T, n // (J * P), J, P).transpose(0, 2, 4, 3, 1).reshape(n // T, n // (J * P), P, J * T),
        "w_l0": a["L0_gnn_W"],
        "ffn_wT": a["L0_ffn_weight"].T,
        "ffn_b": a["L0_ffn_bias"],
        "gnn_w": a["L1_gnn_W"],
        "gnn_b": a["L1_gnn_B"],
        "gate_wT": a["L1_ffn_Wg"].T,
        "gate_b": a["L1_ffn_bg"],
        "experts": _np.concatenate([
            a["L1_ffn_W1"].transpose(0, 2, 1),
            a["L1_ffn_W2"].reshape(e, d, h // P, P).transpose(0, 3, 2, 1).reshape(e, P, h // P * d),
            a["L1_ffn_b1"].reshape(e, h // P, P).transpose(0, 2, 1)], axis=2),
        "b2": a["L1_ffn_b2"],
    }
    nc = _bacc.Bacc("TRN2", target_bir_lowering=False, num_devices=1)
    arrays, args = {}, []
    for name, v in laid.items():
        v = _np.ascontiguousarray(v)
        arrays[f"in_{name}"] = v
        args.append(nc.dram_tensor(f"in_{name}", v.shape, _mybir.dt.from_np(v.dtype), kind="ExternalInput").ap())
    out = nc.dram_tensor("out_0", (n, d), _mybir.dt.from_np(a["x"].dtype), kind="ExternalOutput").ap()
    gnn_ffn_gnn_moe_kernel(nc, *args, out)
    r = _run(nc, [arrays], core_ids=[0])
    return r.results[0]["out_0"]
```
